# Optimizing a Trainium2 kernel written in Bass

```python
import numpy as np
import jax
import jax.numpy as jnp

def _softmax(x, axis=-1):
    return jax.nn.softmax(x, axis=axis)

def _gelu(x):
    return jax.nn.gelu(x, approximate=True)

def _silu(x):
    return jax.nn.silu(x)

def _sigmoid(x):
    return jax.nn.sigmoid(x)

def _layernorm(x, axis=-1, eps=1e-05):
    m = jnp.mean(x, axis=axis, keepdims=True)
    v = jnp.var(x, axis=axis, keepdims=True)
    return (x - m) / jnp.sqrt(v + eps)

def _scatter_add(tgt, idx, src, axis=0):
    return tgt.at[idx].add(src)

def _segment_sum(src, seg, n):
    return jax.ops.segment_sum(src, seg, n)
kernel_name = 'mk_gnn_resnorm_d4_gnn_r32_bc5612'

def setup_inputs(seed: int=0):
    np.random.seed(seed)
    _w = jnp.asarray

    def _rec_inputs():
        import jax
        import jax.numpy as jnp
        _gk = jax.random.key(seed)
        x = -0.0002117 + 1 * jax.random.normal(jax.random.fold_in(_gk, 1), (3125, 256), jnp.float32)
        src = jax.random.randint(jax.random.fold_in(_gk, 2), (50000,), 0, 3125, jnp.int32)
        dst = jnp.minimum((3125 * jax.random.uniform(jax.random.fold_in(_gk, 3), (50000,)) ** 2.0).astype(jnp.int32), 99999)
        _o = jnp.argsort(dst, stable=True)
        src = src[_o]
        dst = dst[_o]
        edge_type_200 = jax.random.randint(jax.random.fold_in(_gk, 13), (50000,), 0, 200, jnp.int32)
        edge_type_8 = jax.random.randint(jax.random.fold_in(_gk, 14), (50000,), 0, 8, jnp.int32)
        return (x, src, dst, edge_type_200, edge_type_8)
    x, src, dst, edge_type_200, edge_type_8 = _rec_inputs()

    def _L0_gnn_setup():
        import jax, jax.numpy as jnp
        import numpy as np
        N_NODES = 3125
        N_EDGES = 100000
        D = 256
        N_LAYERS = 3

        def gcn_layer(x, src, dst, deg_inv_sqrt, W, b):
            h = x @ W
            norm = deg_inv_sqrt[src] * deg_inv_sqrt[dst]
            msg = h[src] * norm[:, None]
            out = jax.ops.segment_sum(msg, dst, num_segments=N_NODES)
            return out + b
        key = jax.random.key(seed)
        ks = jax.random.split(key, 2 + 2 * N_LAYERS)
        x = jax.random.normal(ks[0], (N_NODES, D), dtype=jnp.float32)
        edge_index = jax.random.randint(ks[1], (2, N_EDGES), 0, N_NODES, dtype=jnp.int64)
        inp = {'x': x, 'edge_index': edge_index}
        for i in range(N_LAYERS):
            limit = np.sqrt(6.0 / (D + D)).astype(np.float32)
            inp[f'W{i + 1}'] = jax.random.uniform(ks[2 + 2 * i], (D, D), dtype=jnp.float32, minval=-limit, maxval=limit)
            inp[f'b{i + 1}'] = jnp.zeros((D,), dtype=jnp.float32)
        return inp
    _L0_gnn_all = _L0_gnn_setup()
    _L0_gnn_in = {k: v for k, v in _L0_gnn_all.items() if k in ('W1', 'b1', 'W2', 'b2', 'W3', 'b3')}
    del _L0_gnn_all

    def _L1_gnn_setup():
        import jax, jax.numpy as jnp
        import numpy as np
        N_NODES = 625
        N_EDGES = 10000
        NUM_RELS = 8
        DIM = 256
        BN_EPS = 1e-05
        key = jax.random.key(seed)
        k1, k2, k3, k4, k5 = jax.random.split(key, 5)
        h = jax.random.normal(k1, (N_NODES, DIM), dtype=jnp.float32)
        weight = jax.random.normal(k2, (NUM_RELS, DIM, DIM), dtype=jnp.float32) * 0.05
        gamma = jnp.ones((DIM,), dtype=jnp.float32)
        beta = jnp.zeros((DIM,), dtype=jnp.float32)
        src = jax.random.randint(k3, (N_EDGES,), 0, N_NODES, dtype=jnp.int32)
        dst = jax.random.randint(k4, (N_EDGES,), 0, N_NODES, dtype=jnp.int32)
        rel = jax.random.randint(k5, (N_EDGES,), 0, NUM_RELS, dtype=jnp.int32)
        return {'h': h, 'weight': weight, 'gamma': gamma, 'beta': beta, 'src': src, 'dst': dst, 'rel': rel}
    _L1_gnn_all = _L1_gnn_setup()
    _L1_gnn_in = {k: v for k, v in _L1_gnn_all.items() if k in ('weight', 'gamma', 'beta')}
    del _L1_gnn_all

    def _L2_gnn_setup():
        import jax, jax.numpy as jnp
        import numpy as np
        N_NODES = 3125
        N_EDGES = 50000
        D = 256

        def _sage_layer(x, src, dst, inv_deg, W_self, W_neigh, b):
            agg = jax.ops.segment_sum(x[src], dst, num_segments=N_NODES)
            mean = agg * inv_deg[:, None]
            return x @ W_self + mean @ W_neigh + b
        key = jax.random.key(seed)
        ks = jax.random.split(key, 16)
        inp = {'features': jax.random.normal(ks[0], (N_NODES, D), dtype=jnp.float32), 'src': jax.random.randint(ks[1], (N_EDGES,), 0, N_NODES, dtype=jnp.int32), 'dst': jax.random.randint(ks[2], (N_EDGES,), 0, N_NODES, dtype=jnp.int32)}
        scale = 1.0 / np.sqrt(D)
        for i in range(3):
            inp[f'W{i}_self'] = jax.random.normal(ks[3 + 4 * i], (D, D), dtype=jnp.float32) * scale
            inp[f'W{i}_neigh'] = jax.random.normal(ks[4 + 4 * i], (D, D), dtype=jnp.float32) * scale
            inp[f'b{i}'] = jnp.zeros((D,), dtype=jnp.float32)
        return inp
    _L2_gnn_all = _L2_gnn_setup()
    _L2_gnn_in = {k: v for k, v in _L2_gnn_all.items() if k in ('W0_self', 'W0_neigh', 'b0', 'W1_self', 'W1_neigh', 'b1', 'W2_self', 'W2_neigh', 'b2')}
    del _L2_gnn_all

    def _L3_gnn_setup():
        import jax, jax.numpy as jnp
        import numpy as np
        N, D, E, R = (50000, 256, 20000, 200)
        if __name__ == '__main__':
            out = reference(**setup_inputs())
            print(out.shape, out.dtype)
        key = jax.random.key(seed)
        ks = jax.random.split(key, 12)

        def xavier(k, shape, gain=np.sqrt(2.0)):
            fan_in, fan_out = (shape[0], shape[1])
            bound = gain * np.sqrt(6.0 / (fan_in + fan_out))
            return jax.random.uniform(k, shape, jnp.float32, -bound, bound)
        return {'h': jax.random.normal(ks[0], (N, D), jnp.float32), 'rel_emb': jax.random.normal(ks[1], (R, D), jnp.float32) * 0.1, 'weight_neighbor': xavier(ks[2], (D, D)), 'a': xavier(ks[3], (3 * D, 1)), 'W3': xavier(ks[4], (3 * D, 3 * D)), 'loop_weight': xavier(ks[5], (D, D)), 'evolve_loop_weight': xavier(ks[6], (D, D)), 'src': jax.random.randint(ks[7], (E,), 0, N, jnp.int32), 'dst': jax.random.randint(ks[8], (E,), 0, N, jnp.int32), 'etype': jax.random.randint(ks[9], (E,), 0, R, jnp.int32)}
    _L3_gnn_all = _L3_gnn_setup()
    _L3_gnn_in = {k: v for k, v in _L3_gnn_all.items() if k in ('rel_emb', 'weight_neighbor', 'a', 'W3', 'loop_weight', 'evolve_loop_weight')}
    del _L3_gnn_all
    return {'x': x, 'src': src, 'dst': dst, 'edge_type_200': edge_type_200, 'edge_type_8': edge_type_8, 'L0_gnn_W1': _L0_gnn_in['W1'], 'L0_gnn_b1': _L0_gnn_in['b1'], 'L0_gnn_W2': _L0_gnn_in['W2'], 'L0_gnn_b2': _L0_gnn_in['b2'], 'L0_gnn_W3': _L0_gnn_in['W3'], 'L0_gnn_b3': _L0_gnn_in['b3'], 'L1_gnn_weight': _L1_gnn_in['weight'], 'L1_gnn_gamma': _L1_gnn_in['gamma'], 'L1_gnn_beta': _L1_gnn_in['beta'], 'L2_gnn_W0_self': _L2_gnn_in['W0_self'], 'L2_gnn_W0_neigh': _L2_gnn_in['W0_neigh'], 'L2_gnn_b0': _L2_gnn_in['b0'], 'L2_gnn_W1_self': _L2_gnn_in['W1_self'], 'L2_gnn_W1_neigh': _L2_gnn_in['W1_neigh'], 'L2_gnn_b1': _L2_gnn_in['b1'], 'L2_gnn_W2_self': _L2_gnn_in['W2_self'], 'L2_gnn_W2_neigh': _L2_gnn_in['W2_neigh'], 'L2_gnn_b2': _L2_gnn_in['b2'], 'L3_gnn_rel_emb': _L3_gnn_in['rel_emb'], 'L3_gnn_weight_neighbor': _L3_gnn_in['weight_neighbor'], 'L3_gnn_a': _L3_gnn_in['a'], 'L3_gnn_W3': _L3_gnn_in['W3'], 'L3_gnn_loop_weight': _L3_gnn_in['loop_weight'], 'L3_gnn_evolve_loop_weight': _L3_gnn_in['evolve_loop_weight']}

def reference(x, src, dst, edge_type_200, edge_type_8, L0_gnn_W1, L0_gnn_b1, L0_gnn_W2, L0_gnn_b2, L0_gnn_W3, L0_gnn_b3, L1_gnn_weight, L1_gnn_gamma, L1_gnn_beta, L2_gnn_W0_self, L2_gnn_W0_neigh, L2_gnn_b0, L2_gnn_W1_self, L2_gnn_W1_neigh, L2_gnn_b1, L2_gnn_W2_self, L2_gnn_W2_neigh, L2_gnn_b2, L3_gnn_rel_emb, L3_gnn_weight_neighbor, L3_gnn_a, L3_gnn_W3, L3_gnn_loop_weight, L3_gnn_evolve_loop_weight):
    import jax
    import jax.numpy as jnp

    def _L0_gnn_ref(x, edge_index, W1, b1, W2, b2, W3, b3):
        import jax, jax.numpy as jnp
        import numpy as np
        N_NODES = 3125
        N_EDGES = 100000
        D = 256
        N_LAYERS = 3

        def gcn_layer(x, src, dst, deg_inv_sqrt, W, b):
            h = x @ W
            norm = deg_inv_sqrt[src] * deg_inv_sqrt[dst]
            msg = h[src] * norm[:, None]
            out = jax.ops.segment_sum(msg, dst, num_segments=N_NODES)
            return out + b
        loops = jnp.arange(N_NODES, dtype=edge_index.dtype)
        src = jnp.concatenate([edge_index[0], loops])
        dst = jnp.concatenate([edge_index[1], loops])
        deg = jax.ops.segment_sum(jnp.ones_like(dst, dtype=x.dtype), dst, num_segments=N_NODES)
        deg_inv_sqrt = jnp.where(deg > 0, jax.lax.rsqrt(jnp.maximum(deg, 1e-12)), 0.0)
        for W, b in ((W1, b1), (W2, b2), (W3, b3)):
            x = gcn_layer(x, src, dst, deg_inv_sqrt, W, b)
        return x

    def _L1_gnn_ref(h, weight, gamma, beta, src, dst, rel):
        import jax, jax.numpy as jnp
        import numpy as np
        N_NODES = 625
        N_EDGES = 10000
        NUM_RELS = 8
        DIM = 256
        BN_EPS = 1e-05
        all_h = jnp.einsum('ni,rio->nro', h, weight)
        msg = all_h[src, rel]
        agg = jax.ops.segment_sum(msg, dst, num_segments=h.shape[0])
        mean = jnp.mean(agg, axis=0)
        var = jnp.mean(jnp.square(agg - mean), axis=0)
        out = (agg - mean) * jax.lax.rsqrt(var + BN_EPS) * gamma + beta
        return out

    def _L2_gnn_ref(features, src, dst, W0_self, W0_neigh, b0, W1_self, W1_neigh, b1, W2_self, W2_neigh, b2):
        import jax, jax.numpy as jnp
        import numpy as np
        N_NODES = 3125
        N_EDGES = 50000
        D = 256

        def _sage_layer(x, src, dst, inv_deg, W_self, W_neigh, b):
            agg = jax.ops.segment_sum(x[src], dst, num_segments=N_NODES)
            mean = agg * inv_deg[:, None]
            return x @ W_self + mean @ W_neigh + b
        deg = jax.ops.segment_sum(jnp.ones_like(src, dtype=features.dtype), dst, num_segments=N_NODES)
        inv_deg = 1.0 / jnp.maximum(deg, 1.0)
        h = _sage_layer(features, src, dst, inv_deg, W0_self, W0_neigh, b0)
        h = jax.nn.relu(h)
        h = _sage_layer(h, src, dst, inv_deg, W1_self, W1_neigh, b1)
        h = jax.nn.relu(h)
        h = _sage_layer(h, src, dst, inv_deg, W2_self, W2_neigh, b2)
        return h

    def _L3_gnn_ref(h, rel_emb, weight_neighbor, a, W3, loop_weight, evolve_loop_weight, src, dst, etype):
        import jax, jax.numpy as jnp
        import numpy as np
        N, D, E, R = (50000, 256, 20000, 200)
        if __name__ == '__main__':
            out = reference(**setup_inputs())
            print(out.shape, out.dtype)
        n, d = h.shape
        e = src.shape[0]
        in_deg = jax.ops.segment_sum(jnp.ones((e,), h.dtype), dst, num_segments=n)
        loop_message = jnp.where((in_deg > 0)[:, None], h @ loop_weight, h @ evolve_loop_weight)
        W = (W3 @ a)[:, 0]
        w_src, w_dst, w_rel = (W[:d], W[d:2 * d], W[2 * d:])
        rel_e = rel_emb[etype]
        score = h[src] @ w_src + h[dst] @ w_dst + rel_e @ w_rel
        alpha = jnp.exp(jax.nn.leaky_relu(score))[:, None]
        alpha = alpha / jnp.sum(alpha, axis=1, keepdims=True)
        msg = (h[src] + rel_e) @ weight_neighbor * alpha
        agg = jax.ops.segment_sum(msg, dst, num_segments=n)
        node_repr = jax.nn.relu(agg) + loop_message
        return node_repr
    edge_index = jnp.stack([src, dst])
    x = _layernorm(x + _L0_gnn_ref(x, edge_index, L0_gnn_W1, L0_gnn_b1, L0_gnn_W2, L0_gnn_b2, L0_gnn_W3, L0_gnn_b3), axis=-1)
    x = _layernorm(x + _L1_gnn_ref(x, L1_gnn_weight, L1_gnn_gamma, L1_gnn_beta, src, dst, edge_type_8), axis=-1)
    x = _layernorm(x + _L2_gnn_ref(x, src, dst, L2_gnn_W0_self, L2_gnn_W0_neigh, L2_gnn_b0, L2_gnn_W1_self, L2_gnn_W1_neigh, L2_gnn_b1, L2_gnn_W2_self, L2_gnn_W2_neigh, L2_gnn_b2), axis=-1)
    x = _layernorm(x + _L3_gnn_ref(x, L3_gnn_rel_emb, L3_gnn_weight_neighbor, L3_gnn_a, L3_gnn_W3, L3_gnn_loop_weight, L3_gnn_evolve_loop_weight, src, dst, edge_type_200), axis=-1)
    return x

_drawn_inputs = setup_inputs


def setup_inputs(seed=0):
    import zlib

    import numpy as np

    out = dict(_drawn_inputs(seed))
    spreads = {'L0_gnn_b1': (0.0, 0.1),
     'L0_gnn_b2': (0.0, 0.1),
     'L0_gnn_b3': (0.0, 0.1),
     'L1_gnn_gamma': (1.0, 0.2),
     'L1_gnn_beta': (0.0, 0.1),
     'L2_gnn_b0': (0.0, 0.1),
     'L2_gnn_b1': (0.0, 0.1),
     'L2_gnn_b2': (0.0, 0.1)}
    factors = {}
    for name, (base, spread) in spreads.items():
        noise = np.random.default_rng([zlib.crc32(name.encode()), seed]).standard_normal(out[name].shape)
        drawn = base * np.exp(spread * noise) if base else spread * noise
        out[name] = jnp.asarray(drawn.astype(out[name].dtype))
    for name, factor in factors.items():
        out[name] = (out[name] * factor).astype(out[name].dtype)
    return out
```

```python
import concourse.bass as bass
from concourse import mybir
from contextlib import ExitStack

F32 = mybir.dt.float32
BF16 = mybir.dt.bfloat16
I32 = mybir.dt.int32
ALU = mybir.AluOpType
ACT = mybir.ActivationFunctionType
AX = mybir.AxisListType

P = 128
N = 3125
D = 256
E = 50000
NT = -(-N // P)
LAST = N - (NT - 1) * P
NC = -(-E // P)
EP = NC * P
NREL = 8
R = 200
EPS = 1e-5
PAD_DST = 8000
NI = NC + NT
NIP = 512
GRP = 8
NG = NI // GRP
UN = 5
assert NG % 4 == 0 and NT % UN == 0


class Count:

    def __init__(self, ctx, nc, name):
        self.sem = ctx.enter_context(nc.semaphore(name))
        self.n = 0


class Chain:

    def __init__(self, eng, count):
        self.eng, self.count = eng, count

    def inc(self, ins, times=1):
        ins.then_inc(self.count.sem, 1)
        self.count.n += times

    def wait(self):
        self.eng.wait_ge(self.count.sem, self.count.n)

    def step(self, ins):
        self.inc(ins)
        self.wait()


class Core:
    pass


def allocate(nc, ctx, c):
    def sb(name, shape, dt=F32):
        return ctx.enter_context(nc.sbuf_tensor(name, shape, dt))

    def sem(name):
        return Count(ctx, nc, name)

    c.x = sb("x_res", [P, NT, D])
    c.h = sb("h_cur", [P, NT, D])
    c.acc = sb("acc", [P, NT, D + R])
    c.accd = c.acc[:, :, 0:D]
    c.col_dst = sb("col_dst", [P, NIP])
    c.col_src = sb("col_src", [P, NIP], I32)
    c.col_src8 = sb("col_src8", [P, NIP], I32)
    c.col_et = sb("col_et", [P, NIP])
    c.tile_row = sb("tile_row", [P, NIP], I32)
    c.deg = sb("deg", [P, NT])
    c.dinv = sb("dinv", [P, NT])
    c.ideg = sb("ideg", [P, NT])
    c.has_in = sb("has_in", [P, NT])
    c.ident = sb("ident", [P, P])
    c.ones = sb("ones", [P, P])
    c.lane = sb("lane", [P, P])
    c.gat = sb("gat", [P, 2 * GRP, D + 4])
    c.stage = sb("stage", [P, 4 * GRP], I32)
    c.sel = sb("sel", [P, 2 * GRP, P])
    c.xs = sb("xs", [P, UN, D])
    c.xt = sb("xt", [P, UN, D])
    c.tmp = sb("tmp", [P, UN, D])
    c.w = sb("w", [P, 2, NREL * D])
    c.bias = sb("bias", [P, 3, D])
    c.psum = [ctx.enter_context(nc.psum_tensor(f"bank{k}", [P, 512], F32)) for k in range(8)]

    c.node_no = sb("node_no", [P, P])
    c.lane_r = sb("lane_r", [P, R])
    c.valid = sb("valid", [P, P])
    c.mean = sb("mean", [P, D])
    c.gain = sb("gain", [P, D])
    c.stats = sb("stats", [P, NT, 6])
    c.mv = sb("mv", [P, NT, 2])
    c.var = sb("var", [P, NT])
    c.rstd = sb("rstd", [P, NT])
    c.root = sb("root", [P, 2 * D])
    c.xt2 = sb("xt2", [P, UN, 2 * D])

    c.s_load = sem("loaded")
    c.s_dve = sem("dve_chain")
    c.s_pool = sem("pool_chain")
    c.s_pe = sem("pe_chain")
    c.s_store = sem("stored")
    c.s_gat = [sem(f"gathered{k}") for k in range(2 * GRP)]
    c.s_stage = sem("indices_staged")
    c.s_sel = sem("onehots_ready")
    c.s_mm = sem("edge_products_done")
    c.s_add = sem("edge_sums_added")
    c.s_scaled = sem("tile_scaled")
    c.s_tr = sem("tile_transposed")
    c.s_xt = sem("tile_xt_ready")
    c.s_lin = sem("tile_product_done")
    c.s_out = sem("tile_out_ready")

    c.s_odd = sem("odd_banks_out")
    c.s_slot = [sem(f"slot_stored{k}") for k in range(UN)]
    c.s_alpha = sem("alpha_ready")
    c.s_score = sem("scores_ready")
    c.s_rel = sem("relation_steps")

    c.rec = nc.dram_tensor("edge_records", [EP, 4], I32, kind="Internal").ap()
    c.rtab = nc.dram_tensor("relation_table", [NT * P * NREL, D], F32, kind="Internal").ap()
    c.ltab = nc.dram_tensor("scored_table", [NT * P, D + 4], F32, kind="Internal").ap()
    c.tab = nc.dram_tensor("row_table", [NT * P, D], F32, kind="Internal").ap()


def phase_constants_and_planes(nc, c, p):
    load0, dve0, pool0 = c.s_load.n, c.s_dve.n, c.s_pool.n
    planes = [("src", p.src), ("dst", p.dst), ("et8", p.et8), ("et200", p.et200)]
    whole = E // NC
    with nc.Block() as block:

        @block.gpsimd
        def _(pool):
            ch = Chain(pool, c.s_pool)
            for k, (name, plane) in enumerate(planes):
                ch.inc(nc.gpsimd.memset(plane[:, :], PAD_DST if name == "dst" else 0))
            ch.inc(nc.gpsimd.iota(p.edge_no[:, :], [[1, NC]], base=0, channel_multiplier=NC,
                                  allow_small_or_imprecise_dtypes=True))
            ch.inc(nc.gpsimd.iota(c.lane[:, :], [[1, P]], base=0, channel_multiplier=0,
                                  allow_small_or_imprecise_dtypes=True))
            ch.inc(nc.gpsimd.iota(p.part_no[:, :], [[1, 1]], base=0, channel_multiplier=1,
                                  allow_small_or_imprecise_dtypes=True))
            ch.inc(nc.gpsimd.memset(c.ones[:, :], 1.0))
            ch.inc(nc.gpsimd.memset(p.zero[:, :], 0.0))

        @block.sync
        def _(sp):
            sp.wait_ge(c.s_pool.sem, pool0 + 4)
            for k, (name, plane) in enumerate(planes):
                src = c.ins[name]
                sp.dma_start(plane[0:whole, :], src[0:whole * NC].rearrange("(p j) -> p j", j=NC)
                             ).then_inc(c.s_load.sem, 16)
                sp.dma_start(plane[whole:whole + 1, 0:E - whole * NC],
                             src[whole * NC:E].rearrange("(o j) -> o j", o=1)).then_inc(c.s_load.sem, 16)
            sp.dma_start(c.x[:, 0:NT - 1, :], c.ins["x"][0:(NT - 1) * P, :].rearrange("(t p) d -> p t d", p=P)
                         ).then_inc(c.s_load.sem, 16)
            sp.dma_start(c.x[0:LAST, NT - 1, :], c.ins["x"][(NT - 1) * P:N, :]).then_inc(c.s_load.sem, 16)

        @block.vector
        def _(dve):
            ch = Chain(dve, c.s_dve)
            v = nc.vector
            dve.wait_ge(c.s_pool.sem, pool0 + 9)
            ch.inc(v.tensor_scalar(c.ident[:, :], c.lane[:, :], p.part_no[:, 0:1], None, ALU.is_equal))
            ch.inc(v.tensor_scalar(p.lower[:, :], c.lane[:, :], p.part_no[:, 0:1], None, ALU.is_gt))
            dve.wait_ge(c.s_load.sem, load0 + 160)
            ch.step(v.tensor_single_scalar(p.hi_i[:, :], p.dst[:, :], 7, ALU.arith_shift_right))
            ch.step(v.tensor_scalar(p.hi[:, :], p.hi_i[:, :], float(NT), None, ALU.min))
            ch.step(v.tensor_tensor(p.inb[:, :, :], p.hi[:, :].unsqueeze(1).broadcast_to([P, NT + 1, NC]),
                                    c.lane[:, 0:NT + 1].unsqueeze(2).broadcast_to([P, NT + 1, NC]), ALU.is_equal))
            flat = p.inb[:, :, :].rearrange("p t j -> p (t j)")
            ch.step(v.tensor_tensor_scan(p.run[:, :, :].rearrange("p t j -> p (t j)"),
                                         p.zero[:, 0:1].broadcast_to([P, (NT + 1) * NC]), flat, 0.0,
                                         ALU.add, ALU.add))
            ch.inc(v.memset(p.before[:, 0:1], 0.0))
            ch.step(v.tensor_copy(p.before[:, 1:NT + 2], p.run[:, :, NC - 1]))
            ch.step(v.tensor_tensor(p.cnt[:, :], p.before[:, 1:NT + 2], p.before[:, 0:NT + 1], ALU.subtract))

        @block.tensor
        def _(pe):
            pe.wait_ge(c.s_dve.sem, c.s_dve.n)
            nc.tensor.matmul(c.psum[0][:, 0:NT + 1], p.lower[:, :], p.cnt[:, :], start=True, stop=True)
            nc.tensor.matmul(c.psum[1][:, 0:NT + 1], c.ones[:, :], p.cnt[:, :], start=True, stop=True
                             ).then_inc(c.s_pe.sem, 1)
    c.s_pool.n = pool0 + 9
    c.s_load.n = load0 + 160
    c.s_pe.n += 1

    with nc.Block() as block:
        pe1 = c.s_pe.n

        @block.vector
        def _(dve):
            ch = Chain(dve, c.s_dve)
            v = nc.vector
            nb = NT + 1
            ch.inc(v.memset(p.base[:, 0:1], 0.0))
            ch.step(v.tensor_tensor_scan(p.base[:, 1:nb + 1], p.zero[:, 0:1].broadcast_to([P, nb]),
                                         c.psum[1][:, 0:nb], 0.0, ALU.add, ALU.add))
            ch.step(v.tensor_tensor(p.corr[:, :], p.base[:, 0:nb], c.psum[0][:, 0:nb], ALU.add))
            ch.step(v.tensor_tensor(p.corr[:, :], p.corr[:, :], p.before[:, 0:nb], ALU.subtract))
            ch.step(v.tensor_scalar(p.corr[:, :], p.corr[:, :], -1.0, None, ALU.add))
            ch.step(v.tensor_tensor(p.run[:, :, :], p.run[:, :, :],
                                    p.corr[:, :].unsqueeze(2).broadcast_to([P, nb, NC]), ALU.add))
            ch.step(v.tensor_tensor(p.run[:, :, :], p.run[:, :, :], p.inb[:, :, :], ALU.mult))
            ch.step(v.tensor_reduce(p.place[:, :], p.run[:, :, :].rearrange("p t j -> p j t"), AX.X, ALU.add))
            ch.inc(v.tensor_copy(p.place_i[:, :], p.place[:, :]))
            for k, plane in enumerate((p.src, p.dst, p.et8, p.et200)):
                ch.inc(v.tensor_copy(p.rec_sb[:, :, k], plane[:, :]))
            ch.step(v.tensor_tensor(p.off[:, :], p.place[:, :], p.edge_no[:, :], ALU.not_equal))
            ch.step(v.tensor_reduce(p.moved[:, 0:1], p.off[:, :], AX.X, ALU.add))

        @block.tensor
        def _(pe):
            pe.wait_ge(c.s_dve.sem, c.s_dve.n)
            nc.tensor.matmul(c.psum[2][:, 0:1], c.ones[:, :], p.moved[:, 0:1], start=True, stop=True
                             ).then_inc(c.s_pe.sem, 1)
    c.s_pe.n += 1

    with nc.Block() as block:
        dve1, pool1 = c.s_dve.n, c.s_pool.n

        @block.vector
        def _(dve):
            ch = Chain(dve, c.s_dve)
            ch.step(nc.vector.tensor_scalar(p.flag[:, 0:1], c.psum[2][:, 0:1], 1.0, None, ALU.min))

        @block.gpsimd
        def _(pool):
            rec_out = c.rec.rearrange("(p j) k -> p (j k)", j=NC)
            pool.wait_ge(c.s_dve.sem, dve1 + 1)
            flag = pool.value_load(p.flag[0:1, 0:1], min_val=0, max_val=1)
            cond = pool.If(flag == 0)
            with cond:
                pool.dma_start(rec_out, p.rec_sb[:, :, :].rearrange("p j k -> p (j k)")
                               ).then_inc(c.s_copied.sem, 16)
                pool.wait_ge(c.s_copied.sem, 16)
            with pool.Else():
                with pool.Fori(0, NC) as j:
                    nc.gpsimd.tensor_copy(p.one_place[:, 0:1], p.place_i[:, bass.ds(j, 1)])
                    nc.gpsimd.tensor_copy(p.one_rec[:, :], p.rec_sb[:, bass.ds(j, 1), :]
                                          .rearrange("p o k -> p (o k)")).then_inc(c.s_rec.sem, 1)
                    pool.wait_ge(c.s_rec.sem, j + 1)
                    nc.gpsimd.tensor_tensor(p.spare[:, 0:1], p.place_i[:, 0:1], p.place_i[:, 0:1], ALU.add)
                    nc.gpsimd.indirect_dma_start(c.rec, bass.IndirectOffsetOnAxis(p.one_place[:, 0:1], 0),
                                                 p.one_rec[:, :], None).then_inc(c.s_scat.sem, 16)
                    pool.wait_ge(c.s_scat.sem, j * 16 + 16)


def phase_visits(nc, c, p):
    NQ = NIP // P
    NLO = 17
    assert NC % NLO == 0
    load0, dve0, pool0, pe0 = c.s_load.n, c.s_dve.n, c.s_pool.n, c.s_pe.n
    tail = NC - (NQ - 1) * P
    with nc.Block() as block:

        @block.gpsimd
        def _(pool):
            ch = Chain(pool, c.s_pool)
            ch.inc(nc.gpsimd.memset(p.last_dst[:, :], 0))
            ch.inc(nc.gpsimd.iota(p.visit_no[:, :], [[1, NIP]], base=0, channel_multiplier=0,
                                  allow_small_or_imprecise_dtypes=True))
            ch.inc(nc.gpsimd.iota(p.chunk_no[:, :], [[P, NQ]], base=0, channel_multiplier=1,
                                  allow_small_or_imprecise_dtypes=True))

        @block.sync
        def _(sp):
            sp.wait_ge(c.s_pool.sem, pool0 + 1)
            ends = c.rec.rearrange("(j e) k -> j (e k)", e=P)
            with nc.allow_non_contiguous_dma(reason="one word per chunk"):
                for q in range(NQ):
                    rows = P if q < NQ - 1 else tail
                    sp.dma_start(p.last_dst[0:rows, q:q + 1], ends[q * P:q * P + rows, 4 * (P - 1) + 1:4 * (P - 1) + 2]
                                 ).then_inc(c.s_load.sem, 16)

        @block.vector
        def _(dve):
            ch = Chain(dve, c.s_dve)
            v = nc.vector
            ch.step(v.tensor_single_scalar(p.hi_i[:, :], p.dst[:, :], P - 1, ALU.bitwise_and))
            ch.step(v.tensor_copy(p.lo[:, :], p.hi_i[:, :]))
            def onehots(g, slot):
                return v.tensor_tensor(p.lo_hot[:, slot, :, :],
                                       p.lo[:, bass.ds(g * NLO, NLO)].unsqueeze(2).broadcast_to([P, NLO, P]),
                                       c.lane[:, :].unsqueeze(1).broadcast_to([P, NLO, P]), ALU.is_equal)
            for g in range(3):
                if g >= 2:
                    dve.wait_ge(c.s_pe.sem, pe0 + g - 1)
                onehots(g, g % 2).then_inc(c.s_sel.sem, 1)
            with dve.Fori(1, NC // NLO // 2) as it:
                for s in range(2):
                    dve.wait_ge(c.s_pe.sem, pe0 + it * 2 + s)
                    onehots(it * 2 + 1 + s, (1 + s) % 2).then_inc(c.s_sel.sem, 1)

        @block.tensor
        def _(pe):
            def count(g, slot, first, last):
                for k in range(NLO):
                    ins = nc.tensor.matmul(c.psum[7][:, 0:NT], p.lo_hot[:, slot, k, :],
                                           p.inb[:, 0:NT, bass.ds(g * NLO + k, 1)].rearrange("p t o -> p (t o)"),
                                           start=first and k == 0, stop=last and k == NLO - 1,
                                           skip_group_check=True)
                ins.then_inc(c.s_pe.sem, 1)
            pe.wait_ge(c.s_sel.sem, 1)
            count(0, 0, True, False)
            with pe.Fori(0, NC // NLO // 2) as it:
                for s in range(2):
                    pe.wait_ge(c.s_sel.sem, it * 2 + 2 + s)
                    count(it * 2 + 1 + s, (1 + s) % 2, False, False)
    c.s_pool.n += 3
    c.s_load.n += 16 * NQ
    c.s_sel.n += NC // NLO
    c.s_pe.n += NC // NLO

    with nc.Block() as block:

        @block.vector
        def _(dve):
            ch = Chain(dve, c.s_dve)
            v = nc.vector
            dve.wait_ge(c.s_load.sem, c.s_load.n)
            ch.step(v.tensor_single_scalar(p.last_hi[:, :], p.last_dst[:, :], 7, ALU.arith_shift_right))
            ch.inc(v.tensor_scalar(p.past[:, :], p.chunk_no[:, :], float(NC), 1e6, ALU.is_ge, ALU.mult))
            ch.step(v.tensor_scalar(p.leave[:, :], p.last_hi[:, :], float(NT - 1), None, ALU.min))
            ch.step(v.tensor_tensor(p.leave[:, :], p.leave[:, :], p.chunk_no[:, :], ALU.add))
            ch.step(v.tensor_tensor(p.leave[:, :], p.leave[:, :], p.past[:, :], ALU.add))
            for q in range(NQ):
                ch.inc(v.tensor_scalar(p.gone[:, q, :], p.visit_no[:, :], p.leave[:, q:q + 1], None, ALU.is_gt))
            ch.step(v.tensor_copy(c.deg[:, :], c.psum[7][:, 0:NT]))
            ch.inc(v.tensor_scalar(p.deg_loop[:, :], c.deg[:, :], 1.0, None, ALU.add))
            ch.inc(v.tensor_scalar(c.has_in[:, :], c.deg[:, :], 1.0, None, ALU.min))
            ch.step(v.tensor_scalar(c.ideg[:, :], c.deg[:, :], 1.0, None, ALU.max))
            ch.step(v.reciprocal(c.ideg[:, :], c.ideg[:, :]))

        @block.tensor
        def _(pe):
            pe.wait_ge(c.s_dve.sem, c.s_dve.n)
            for q in range(NQ):
                ins = nc.tensor.matmul(c.psum[0][:, :], c.ones[:, :], p.gone[:, q, :],
                                       start=q == 0, stop=q == NQ - 1)
            ins.then_inc(c.s_pe.sem, 1)
    c.s_pe.n += 1

    with nc.Block() as block:

        @block.vector
        def _(dve):
            ch = Chain(dve, c.s_dve)
            v = nc.vector
            ch.step(v.tensor_scalar(p.chunk_row[:, :], c.psum[0][:, :], float(NC - 1), None, ALU.min))
            ch.step(v.tensor_tensor(p.tile_f[:, :], p.visit_no[:, :], p.chunk_row[:, :], ALU.subtract))
            ch.step(v.tensor_scalar(c.tile_row[:, :], p.tile_f[:, :], float(NT - 1), None, ALU.min))

        @block.tensor
        def _(pe):
            pe.wait_ge(c.s_dve.sem, c.s_dve.n)
            for q in range(NQ):
                ins = nc.tensor.transpose(c.psum[1][:, q * P:(q + 1) * P], p.chunk_row[:, q * P:(q + 1) * P],
                                          c.ident[:, :])
            ins.then_inc(c.s_pe.sem, 1)
    c.s_pe.n += 1

    with nc.Block() as block:
        dve1, load1 = c.s_dve.n, c.s_load.n

        @block.vector
        def _(dve):
            ch = Chain(dve, c.s_dve)
            ch.step(nc.vector.tensor_copy(p.chunk_of[:, :], c.psum[1][:, 0:NQ * P:P]))
            dve.wait_ge(c.s_fetch.sem, 16 * NQ)
            for k in range(4):
                ch.inc(nc.vector.tensor_copy(p.fetched_f[:, :, k, :],
                                             p.fetched[:, :, :].rearrange("p q (e k) -> p q e k", k=4)[:, :, :, k]))

        @block.gpsimd
        def _(pool):
            pool.wait_ge(c.s_dve.sem, dve1 + 1)
            rows = c.rec.rearrange("(j e) k -> j (e k)", e=P)
            for q in range(NQ):
                nc.gpsimd.indirect_dma_start(p.fetched[:, q, :], None, rows,
                                             bass.IndirectOffsetOnAxis(p.chunk_of[:, q:q + 1], 0)
                                             ).then_inc(c.s_fetch.sem, 16)

        @block.tensor
        def _(pe):
            pe.wait_ge(c.s_dve.sem, c.s_dve.n)
            for k in range(4):
                for q in range(NQ):
                    ins = nc.tensor.transpose(c.psum[2 + k][:, q * P:(q + 1) * P], p.fetched_f[:, q, k, :],
                                              c.ident[:, :])
            ins.then_inc(c.s_pe.sem, 1)
    c.s_pe.n += 1

    with nc.Block() as block:

        @block.vector
        def _(dve):
            ch = Chain(dve, c.s_dve)
            v = nc.vector
            src, dst, et8, et200 = c.psum[2], c.psum[3], c.psum[4], c.psum[5]
            ch.inc(v.tensor_copy(c.col_src[:, :], src[:, :]))
            ch.inc(v.tensor_copy(c.col_et[:, :], et200[:, :]))
            ch.inc(v.tensor_copy(p.src_f[:, :], src[:, :]))
            ch.inc(v.tensor_copy(p.dst_f[:, :], dst[:, :]))
            ch.step(v.tensor_scalar(p.first_f[:, :], p.tile_f[:, :], float(P), None, ALU.mult))
            ch.inc(v.tensor_tensor(c.col_dst[:, :], p.dst_f[:, :], p.first_f[:, :], ALU.subtract))
            ch.step(v.tensor_scalar(p.src_f[:, :], p.src_f[:, :], float(NREL), None, ALU.mult))
            ch.step(v.tensor_tensor(p.src_f[:, :], p.src_f[:, :], et8[:, :], ALU.add))
            ch.step(v.tensor_copy(c.col_src8[:, :], p.src_f[:, :]))


def phase_rsqrt(nc, c, out, inp, n):
    dve0, act0 = c.s_dve.n, c.s_scaled.n
    root, sq = c.root[:, 0:n], c.root[:, n:2 * n]
    with nc.Block() as block:

        @block.scalar
        def _(act):
            nc.scalar.activation(root, inp[:, :], ACT.Sqrt).then_inc(c.s_scaled.sem, 1)

        @block.vector
        def _(dve):
            ch = Chain(dve, c.s_dve)
            v = nc.vector
            dve.wait_ge(c.s_scaled.sem, act0 + 1)
            ch.step(v.reciprocal(out[:, :], root))
            for _ in range(2):
                ch.step(v.tensor_tensor(sq, out[:, :], out[:, :], ALU.mult))
                ch.step(v.tensor_tensor(sq, sq, inp[:, :], ALU.mult))
                ch.step(v.tensor_scalar(sq, sq, -0.5, 1.5, ALU.mult, ALU.add))
                ch.step(v.tensor_tensor(out[:, :], out[:, :], sq, ALU.mult))
    c.s_scaled.n += 1


def prepare(nc, c):
    with ExitStack() as ctx:
        p = Core()

        def sb(name, shape, dt=F32):
            return ctx.enter_context(nc.sbuf_tensor(name, shape, dt))

        p.src, p.dst, p.et8, p.et200, p.hi_i, p.place_i = (
            sb("p_" + name, [P, NC], I32) for name in ("src", "dst", "et8", "et200", "hi_i", "place_i"))
        p.hi = sb("p_hi", [P, NC])
        p.lo = p.hi
        p.edge_no = sb("p_edge_no", [P, NC])
        p.part_no = sb("p_part_no", [P, 1])
        p.zero = sb("p_zero", [P, 1])
        p.lower = sb("p_lower", [P, P])
        p.inb = c.h[:, :, :].rearrange("p t d -> p (t d)")[:, 0:(NT + 1) * NC // 2].bitcast(BF16).rearrange(
            "p (t j) -> p t j", j=NC)
        p.run = c.acc[:, :, :].rearrange("p t d -> p (t d)")[:, 0:(NT + 1) * NC].rearrange(
            "p (t j) -> p t j", j=NC)
        p.before = sb("p_before", [P, NT + 2])
        p.cnt = sb("p_cnt", [P, NT + 1])
        p.base = sb("p_base", [P, NT + 2])
        p.corr = sb("p_corr", [P, NT + 1])
        p.place = sb("p_place", [P, NC])
        p.off = sb("p_off", [P, NC])
        p.rec_sb = c.xt2[:, :, :].rearrange("p s d -> p (s d)")[:, 0:4 * NC].bitcast(I32).rearrange("p (j k) -> p j k", k=4)
        p.moved = sb("p_moved", [P, 1])
        p.flag = sb("p_flag", [P, 1], I32)
        p.one_place = sb("p_one_place", [P, 1], I32)
        p.spare = sb("p_spare", [P, 1], I32)
        p.one_rec = sb("p_one_rec", [P, 4], I32)
        c.s_copied = Count(ctx, nc, "records_copied")
        c.s_rec = Count(ctx, nc, "record_staged")
        c.s_scat = Count(ctx, nc, "record_scattered")
        phase_constants_and_planes(nc, c, p)

        p.last_dst = sb("p_last_dst", [P, 4], I32)
        p.last_hi = sb("p_last_hi", [P, 4], I32)
        p.visit_no = sb("p_visit_no", [P, NIP])
        p.chunk_no = sb("p_chunk_no", [P, 4])
        p.past = sb("p_past", [P, 4])
        p.leave = sb("p_leave", [P, 4])
        hf = c.acc[:, :, :].rearrange("p t d -> p (t d)")
        p.lo_hot = hf[:, 0:2 * 17 * P // 2].bitcast(BF16).rearrange("p (s k n) -> p s k n", s=2, k=17)
        p.gone = hf[:, 0:4 * NIP].rearrange("p (q n) -> p q n", q=4)
        p.fetched = hf[:, 2048:4096].bitcast(I32).rearrange("p (q n) -> p q n", q=4)
        p.fetched_f = hf[:, 4096:6144].rearrange("p (q k e) -> p q k e", q=4, k=4)
        p.deg_loop = sb("p_deg_loop", [P, NT])
        p.chunk_row = c.xs[:, 0:2, :].rearrange("p s d -> p (s d)")
        p.tile_f = c.xs[:, 2:4, :].rearrange("p s d -> p (s d)")
        p.chunk_of = sb("p_chunk_of", [P, 4], I32)
        p.src_f = hf[:, 0:NIP]
        p.dst_f = hf[:, NIP:2 * NIP]
        p.first_f = hf[:, 2 * NIP:3 * NIP]
        c.s_fetch = Count(ctx, nc, "chunks_fetched")
        phase_visits(nc, c, p)
        phase_rsqrt(nc, c, c.dinv, p.deg_loop, NT)


def phase_edges(nc, c, table, index):
    st0, sel0, mm0, add0 = c.s_stage.n, c.s_sel.n, c.s_mm.n, c.s_add.n
    gat0 = [s.n for s in c.s_gat]
    with nc.Block() as block:

        @block.gpsimd
        def _(pool):
            def copy_indices(group, slot):
                nc.gpsimd.tensor_copy(c.stage[:, slot * GRP:(slot + 1) * GRP],
                                      index[:, bass.ds(group * GRP, GRP)]).then_inc(c.s_stage.sem, 1)

            def gather(slot, ring):
                for j in range(GRP):
                    nc.gpsimd.indirect_dma_start(
                        c.gat[:, ring * GRP + j, 0:D], None, table,
                        bass.IndirectOffsetOnAxis(c.stage[:, slot * GRP + j:slot * GRP + j + 1], 0)
                    ).then_inc(c.s_gat[ring * GRP + j].sem, 16)

            copy_indices(0, 0)
            copy_indices(1, 1)
            for g in range(4):
                if g >= 2:
                    pool.wait_ge(c.s_mm.sem, mm0 + GRP * (g - 1))
                pool.wait_ge(c.s_stage.sem, st0 + g + 1)
                copy_indices(g + 2, (g + 2) % 4)
                gather(g % 4, g % 2)
            with pool.Fori(1, NG // 4) as it:
                for s in range(4):
                    pool.wait_ge(c.s_mm.sem, it * (4 * GRP) + (mm0 + GRP * (s - 1)))
                    pool.wait_ge(c.s_stage.sem, it * 4 + (st0 + s + 1))
                    copy_indices(it * 4 + (s + 2), (s + 2) % 4)
                    gather(s, s % 2)

        @block.vector
        def _(dve):
            def onehot(visit, slot):
                nc.vector.tensor_scalar(c.sel[:, slot, :], c.lane[:, :], c.col_dst[:, bass.ds(visit, 1)], None,
                                        ALU.is_equal).then_inc(c.s_sel.sem, 1)

            for j in range(GRP):
                onehot(j, j)

            def group(g, ring):
                tiles = [dve.value_load(c.tile_row[0:1, bass.ds(g * GRP + j, 1)], min_val=0, max_val=NT - 1)
                         for j in range(GRP)]
                for j in range(GRP):
                    onehot(g * GRP + (GRP + j), (1 - ring) * GRP + j)
                    dve.wait_ge(c.s_mm.sem, g * GRP + (mm0 + j + 1))
                    dve.wait_ge(c.s_add.sem, g * GRP + (add0 + j))
                    into = c.acc[:, bass.ds(tiles[j], 1), 0:D].rearrange("p o d -> p (o d)")
                    nc.vector.tensor_tensor(into, into, c.psum[j][:, 0:D], ALU.add).then_inc(c.s_add.sem, 1)

            with dve.Fori(0, NG // 2) as it:
                for ring in range(2):
                    group(it * 2 + ring, ring)

        @block.tensor
        def _(pe):
            def group(g, ring, turn, first):
                pe.wait_ge(c.s_sel.sem, g * GRP + (sel0 + GRP))
                for j in range(GRP):
                    k = ring * GRP + j
                    pe.wait_ge(c.s_gat[k].sem, turn * 16 + (gat0[k] + 16))
                    if not first:
                        pe.wait_ge(c.s_add.sem, g * GRP + (add0 + j + 1 - GRP))
                    nc.tensor.matmul(c.psum[j][:, 0:D], c.sel[:, k, :], c.gat[:, k, 0:D], start=True, stop=True
                                     ).then_inc(c.s_mm.sem, 1)
            group(0, 0, 0, True)
            group(1, 1, 0, False)
            with pe.Fori(1, NG // 2) as it:
                for ring in range(2):
                    group(it * 2 + ring, ring, it, False)
    c.s_stage.n += NG + 2
    c.s_sel.n += NI + GRP
    c.s_mm.n += NI
    c.s_add.n += NI
    for s in c.s_gat:
        s.n += 16 * NG // 2


def phase_load(nc, c, loads):
    with nc.Block() as block:

        @block.sync
        def _(sp):
            for dst, src in loads:
                sp.dma_start(dst, src).then_inc(c.s_load.sem, 16)
            sp.wait_ge(c.s_load.sem, c.s_load.n + 16 * len(loads))
    c.s_load.n += 16 * len(loads)


def halves(w):
    return w.rearrange("(k p) n -> p k n", p=P)


def each_tile(eng, body):
    with eng.Fori(0, NT // UN) as it:
        for s in range(UN):
            body(it * UN + s, s)


def tile_of(ap, t):
    return ap[:, bass.ds(t, 1), :].rearrange("p o d -> p (o d)")


def col_of(ap, t):
    return ap[:, bass.ds(t, 1)]


def phase_gcn_linear(nc, c, source, layer):
    sc0, tr0, xt0, lin0, out0, st0, dve0 = (s.n for s in (c.s_scaled, c.s_tr, c.s_xt, c.s_lin, c.s_out,
                                                          c.s_store, c.s_dve))
    first = layer == 0
    banks_t = [c.psum[s // 2][:, (s % 2) * D:(s % 2 + 1) * D] for s in range(UN)]
    banks_o = [c.psum[3 + s][:, 0:D] for s in range(UN)]
    with nc.Block() as block:

        @block.vector
        def _(dve):
            def body(t, s):
                if not first:
                    nc.vector.scalar_tensor_tensor(tile_of(c.h, t), tile_of(c.accd, t), col_of(c.dinv, t),
                                                   c.bias[:, layer - 1, :], ALU.mult, ALU.add).then_inc(c.s_dve.sem, 1)
            if not first:
                each_tile(dve, body)

            def out(t, s):
                dve.wait_ge(c.s_lin.sem, t + (lin0 + 1))
                nc.vector.tensor_copy(tile_of(c.accd, t), banks_o[s]).then_inc(c.s_out.sem, 1)
            if not first:
                dve.wait_ge(c.s_dve.sem, dve0 + NT)
            each_tile(dve, out)

        @block.scalar
        def _(act):
            src = source if first else c.h

            def scale(t, s, early):
                if not first:
                    act.wait_ge(c.s_dve.sem, t + (dve0 + 1))
                if not early:
                    act.wait_ge(c.s_tr.sem, t + (tr0 + 1 - UN))
                nc.scalar.activation(c.xs[:, s, :], tile_of(src, t), ACT.Copy, scale=col_of(c.dinv, t)
                                     ).then_inc(c.s_scaled.sem, 1)

            def evict(t, s, early):
                act.wait_ge(c.s_tr.sem, t + (tr0 + 1))
                if not early:
                    act.wait_ge(c.s_lin.sem, t + (lin0 + 1 - UN))
                nc.scalar.copy(c.xt[:, s, :], banks_t[s]).then_inc(c.s_xt.sem, 1)

            for s in range(UN):
                scale(s, s, True)
                evict(s, s, True)
            with act.Fori(1, NT // UN) as it:
                for s in range(UN):
                    scale(it * UN + s, s, False)
                    evict(it * UN + s, s, False)

        @block.tensor
        def _(pe):
            def body(t, s, early):
                pe.wait_ge(c.s_scaled.sem, t + (sc0 + 1))
                if not early:
                    pe.wait_ge(c.s_xt.sem, t + (xt0 + 1 - UN))
                for k in range(2):
                    ins = nc.tensor.transpose(banks_t[s][:, k * P:(k + 1) * P], c.xs[:, s, k * P:(k + 1) * P],
                                              c.ident[:, :])
                ins.then_inc(c.s_tr.sem, 1)
                pe.wait_ge(c.s_xt.sem, t + (xt0 + 1))
                if not early:
                    pe.wait_ge(c.s_out.sem, t + (out0 + 1 - UN))
                for k in range(2):
                    ins = nc.tensor.matmul(banks_o[s], c.xt[:, s, k * P:(k + 1) * P], c.w[:, k, 0:D],
                                           start=k == 0, stop=k == 1)
                ins.then_inc(c.s_lin.sem, 1)
            for s in range(UN):
                body(s, s, True)
            with pe.Fori(1, NT // UN) as it:
                for s in range(UN):
                    body(it * UN + s, s, False)

        @block.sync
        def _(sp):
            for g in range(NT // UN):
                sp.wait_ge(c.s_out.sem, out0 + UN * (g + 1))
                sp.dma_start(c.tab[g * UN * P:(g + 1) * UN * P, :].rearrange("(t p) d -> p t d", p=P),
                             c.accd[:, g * UN:(g + 1) * UN, :]).then_inc(c.s_store.sem, 16)
            sp.wait_ge(c.s_store.sem, st0 + 16 * (NT // UN))
    for s in (c.s_scaled, c.s_tr, c.s_xt, c.s_lin, c.s_out):
        s.n += NT
    if not first:
        c.s_dve.n += NT
    c.s_store.n += 16 * (NT // UN)


def sweeps(dve, c, ch):
    def sweep(step):
        with dve.Fori(0, NT // UN) as it:
            for s in range(UN):
                step(it * UN + s, s).then_inc(c.s_dve.sem, 1)
        c.s_dve.n += NT
        ch.wait()
    return sweep


def phase_norm(nc, c, scale, bias):
    with nc.Block() as block:

        @block.vector
        def _(dve):
            v = nc.vector
            ch = Chain(dve, c.s_dve)

            sweep = sweeps(dve, c, ch)
            if scale is not None:
                sweep(lambda t, s: v.scalar_tensor_tensor(tile_of(c.h, t), tile_of(c.accd, t), col_of(scale, t),
                                                          bias, ALU.mult, ALU.add))
            sweep(lambda t, s: v.tensor_tensor(tile_of(c.x, t), tile_of(c.x, t), tile_of(c.h, t), ALU.add))
            sweep(lambda t, s: v.bn_stats(c.stats[:, bass.ds(t, 1), :].rearrange("p o k -> p (o k)"), tile_of(c.x, t)))
            for t in range(NT):
                ch.inc(v.bn_aggr(c.mv[:, t, :], c.stats[:, t, :]))
            ch.wait()
            ch.step(v.tensor_scalar(c.var[:, :], c.mv[:, :, 1], EPS, None, ALU.add))
    phase_rsqrt(nc, c, c.rstd, c.var, NT)
    with nc.Block() as block:

        @block.vector
        def _(dve):
            v = nc.vector
            ch = Chain(dve, c.s_dve)
            sweep = sweeps(dve, c, ch)
            sweep(lambda t, s: v.tensor_scalar(tile_of(c.x, t), tile_of(c.x, t),
                                               c.mv[:, bass.ds(t, 1), 0:1].rearrange("p o k -> p (o k)"),
                                               col_of(c.rstd, t), ALU.subtract, ALU.mult))


def phase_store(nc, c, out):
    with nc.Block() as block:

        @block.sync
        def _(sp):
            whole = NT - 1
            sp.dma_start(out[0:whole * P, :].rearrange("(t p) d -> p t d", p=P), c.x[:, 0:whole, :]
                         ).then_inc(c.s_store.sem, 16)
            sp.dma_start(out[whole * P:N, :], c.x[0:LAST, whole, :]).then_inc(c.s_store.sem, 16)
            sp.wait_ge(c.s_store.sem, c.s_store.n + 32)
    c.s_store.n += 32


def phase_start(nc, c):
    with nc.Block() as block:

        @block.vector
        def _(dve):
            ch = Chain(dve, c.s_dve)
            ch.step(nc.vector.memset(c.x[:, NT - 1, :], 0.0))
            nc.vector.memset(c.valid[:, :], 0.0).then_inc(c.s_add.sem, 1)

        @block.gpsimd
        def _(pool):
            ch = Chain(pool, c.s_pool)
            ch.inc(nc.gpsimd.iota(c.node_no[:, :], [[0, P]], base=0, channel_multiplier=1,
                                  allow_small_or_imprecise_dtypes=True))
            ch.step(nc.gpsimd.iota(c.lane_r[:, :], [[1, R]], base=0, channel_multiplier=0,
                                   allow_small_or_imprecise_dtypes=True))
    c.s_add.n += 1


def phase_zero(nc, c, width):
    with nc.Block() as block:

        @block.vector
        def _(dve):
            ch = Chain(dve, c.s_dve)
            ch.step(nc.vector.memset(c.acc[:, :, 0:width], 0.0))


def phase_relation_table(nc, c):
    QB = NREL * D // 512
    sc0, tr0, xt0, lin0, out0, st0 = (s.n for s in (c.s_scaled, c.s_tr, c.s_xt, c.s_lin, c.s_out, c.s_store))
    slot0 = [s.n for s in c.s_slot]
    banks_t = [c.psum[s // 2][:, (s % 2) * D:(s % 2 + 1) * D] for s in range(UN)]
    rows = c.acc[:, :, :].rearrange("p t d -> p (t d)")[:, 0:UN * NREL * D].rearrange("p (s n) -> p s n", s=UN)
    dram = c.rtab.rearrange("(n r) d -> n (r d)", r=NREL)
    with nc.Block() as block:

        @block.scalar
        def _(act):
            def body(t, s, early):
                if not early:
                    act.wait_ge(c.s_tr.sem, t + (tr0 + 1 - UN))
                nc.scalar.copy(c.xs[:, s, :], tile_of(c.x, t)).then_inc(c.s_scaled.sem, 1)
                act.wait_ge(c.s_tr.sem, t + (tr0 + 1))
                if not early:
                    act.wait_ge(c.s_lin.sem, t * QB + (lin0 + QB * (1 - UN)))
                nc.scalar.copy(c.xt[:, s, :], banks_t[s]).then_inc(c.s_xt.sem, 1)
                if not early:
                    act.wait_ge(c.s_slot[s].sem, turn_of(t) * 16 + slot0[s])
                for q in range(0, QB, 2):
                    act.wait_ge(c.s_lin.sem, t * QB + (lin0 + q + 1))
                    nc.scalar.copy(rows[:, s, q * 512:(q + 1) * 512], c.psum[3 + q][:, :]).then_inc(c.s_out.sem, 1)

            unrolled(act, body)

        @block.vector
        def _(dve):
            def body(t, s, early):
                if not early:
                    dve.wait_ge(c.s_slot[s].sem, turn_of(t) * 16 + slot0[s])
                for q in range(1, QB, 2):
                    dve.wait_ge(c.s_lin.sem, t * QB + (lin0 + q + 1))
                    nc.vector.tensor_copy(rows[:, s, q * 512:(q + 1) * 512], c.psum[3 + q][:, :]
                                          ).then_inc(c.s_odd.sem, 1)

            unrolled(dve, body)

        @block.tensor
        def _(pe):
            def body(t, s, early):
                pe.wait_ge(c.s_scaled.sem, t + (sc0 + 1))
                if not early:
                    pe.wait_ge(c.s_xt.sem, t + (xt0 + 1 - UN))
                for k in range(2):
                    ins = nc.tensor.transpose(banks_t[s][:, k * P:(k + 1) * P], c.xs[:, s, k * P:(k + 1) * P],
                                              c.ident[:, :])
                ins.then_inc(c.s_tr.sem, 1)
                pe.wait_ge(c.s_xt.sem, t + (xt0 + 1))
                for q in range(QB):
                    if not (early and s == 0):
                        done = (c.s_out, out0) if q % 2 == 0 else (c.s_odd, c.s_odd.n)
                        pe.wait_ge(done[0].sem, t * (QB // 2) + (done[1] + q // 2 + 1 - QB // 2))
                    for k in range(2):
                        ins = nc.tensor.matmul(c.psum[3 + q][:, :], c.xt[:, s, k * P:(k + 1) * P],
                                               c.w[:, k, q * 512:(q + 1) * 512], start=k == 0, stop=k == 1)
                    ins.then_inc(c.s_lin.sem, 1)

            unrolled(pe, body)

        @block.sync
        def _(sp):
            def body(t, s, early):
                sp.wait_ge(c.s_out.sem, t * (QB // 2) + (out0 + QB // 2))
                sp.wait_ge(c.s_odd.sem, t * (QB // 2) + (c.s_odd.n + QB // 2))
                sp.dma_start(dram[t * P:(t + 1) * P, :], rows[:, s, :]).then_inc(c.s_slot[s].sem, 16)

            for t in range(NT):
                body(t, t % UN, False)
            for s in range(UN):
                sp.wait_ge(c.s_slot[s].sem, slot0[s] + 16 * (NT // UN))
    for s in (c.s_scaled, c.s_tr, c.s_xt):
        s.n += NT
    c.s_lin.n += NT * QB
    c.s_out.n += NT * QB // 2
    c.s_odd.n += NT * QB // 2
    for s in c.s_slot:
        s.n += 16 * (NT // UN)


class Turn:
    now = 0


def turn_of(t):
    return Turn.now


def unrolled(eng, body):
    Turn.now = 0
    for s in range(UN):
        body(s, s, True)
    with eng.Fori(1, NT // UN) as it:
        Turn.now = it
        for s in range(UN):
            body(it * UN + s, s, False)


def phase_batch_norm(nc, c):
    pe0, dve0 = c.s_pe.n, c.s_dve.n

    def sums(data, tail):
        with nc.Block() as block:

            @block.tensor
            def _(pe):
                nc.tensor.matmul(c.psum[0][:, 0:D], c.ones[:, :], data[:, 0, :], start=True, stop=False)
                for t in range(1, NT):
                    ins = nc.tensor.matmul(c.psum[0][:, 0:D], tail if t == NT - 1 else c.ones[:, :],
                                           data[:, t, :], start=False, stop=t == NT - 1)
                ins.then_inc(c.s_pe.sem, 1)
        c.s_pe.n += 1

    sums(c.accd, c.ones[:, :])
    with nc.Block() as block:

        @block.vector
        def _(dve):
            v = nc.vector
            ch = Chain(dve, c.s_dve)
            sweep = sweeps(dve, c, ch)
            ch.inc(v.tensor_scalar(c.valid[:, :], c.node_no[:, :], float(LAST), None, ALU.is_lt))
            ch.step(v.tensor_scalar(c.mean[:, :], c.psum[0][:, 0:D], 1.0 / N, None, ALU.mult))
            sweep(lambda t, s: v.tensor_tensor(tile_of(c.accd, t), tile_of(c.accd, t), c.mean[:, :], ALU.subtract))
            sweep(lambda t, s: v.tensor_tensor(tile_of(c.h, t), tile_of(c.accd, t), tile_of(c.accd, t), ALU.mult))
    sums(c.h, c.valid[:, :])
    with nc.Block() as block:

        @block.vector
        def _(dve):
            ch = Chain(dve, c.s_dve)
            ch.step(nc.vector.tensor_scalar(c.mean[:, :], c.psum[0][:, 0:D], 1.0 / N, EPS, ALU.mult, ALU.add))
    phase_rsqrt(nc, c, c.gain, c.mean, D)
    with nc.Block() as block:

        @block.vector
        def _(dve):
            v = nc.vector
            ch = Chain(dve, c.s_dve)
            sweep = sweeps(dve, c, ch)
            ch.step(v.tensor_tensor(c.gain[:, :], c.gain[:, :], c.bias[:, 0, :], ALU.mult))
            sweep(lambda t, s: v.tensor_tensor(tile_of(c.h, t), tile_of(c.accd, t), c.gain[:, :], ALU.mult))
            sweep(lambda t, s: v.tensor_tensor(tile_of(c.h, t), tile_of(c.h, t), c.bias[:, 1, :], ALU.add))


def phase_to_table(nc, c, source, table, width):
    st0 = c.s_store.n
    with nc.Block() as block:

        @block.sync
        def _(sp):
            sp.dma_start(table.rearrange("(t p) d -> p t d", p=P), source).then_inc(c.s_store.sem, 16)
            sp.wait_ge(c.s_store.sem, st0 + 16)

        @block.vector
        def _(dve):
            ch = Chain(dve, c.s_dve)
            if width > D:
                dve.wait_ge(c.s_store.sem, st0 + 16)
            ch.step(nc.vector.memset(c.acc[:, :, 0:width], 0.0))
    c.s_store.n += 16


def phase_sage_linear(nc, c, source, layer):
    sc0, tr0, xt0, lin0, out0, dve0 = (s.n for s in (c.s_scaled, c.s_tr, c.s_xt, c.s_lin, c.s_out, c.s_dve))
    bank_of = [0, 1, 2, 0, 1]
    banks_o = [c.psum[3 + s][:, 0:D] for s in range(UN)]
    with nc.Block() as block:

        @block.vector
        def _(dve):
            def body(t, s, early):
                if not early:
                    dve.wait_ge(c.s_tr.sem, t + (tr0 + 1 - UN))
                nc.vector.tensor_scalar(c.tmp[:, s, :], tile_of(c.accd, t), col_of(c.ideg, t), None, ALU.mult
                                        ).then_inc(c.s_dve.sem, 1)
                dve.wait_ge(c.s_lin.sem, t + (lin0 + 1))
                if layer < 2:
                    nc.vector.tensor_scalar(tile_of(c.h, t), banks_o[s], 0.0, None, ALU.max).then_inc(c.s_out.sem, 1)
                else:
                    nc.vector.tensor_copy(tile_of(c.h, t), banks_o[s]).then_inc(c.s_out.sem, 1)

            unrolled(dve, body)

        @block.scalar
        def _(act):
            def body(t, s, early):
                if not early:
                    act.wait_ge(c.s_tr.sem, t + (tr0 + 1 - UN))
                nc.scalar.copy(c.xs[:, s, :], tile_of(source, t)).then_inc(c.s_scaled.sem, 1)
                act.wait_ge(c.s_tr.sem, t + (tr0 + 1))
                if not early:
                    act.wait_ge(c.s_lin.sem, t + (lin0 + 1 - UN))
                nc.scalar.copy(c.xt2[:, s, :], c.psum[bank_of[s]][:, :]).then_inc(c.s_xt.sem, 1)

            unrolled(act, body)

        @block.tensor
        def _(pe):
            def body(t, s, early):
                pe.wait_ge(c.s_scaled.sem, t + (sc0 + 1))
                pe.wait_ge(c.s_dve.sem, t + (dve0 + 1))
                if not (early and s < 3):
                    pe.wait_ge(c.s_xt.sem, t + (xt0 - 1))
                bank = c.psum[bank_of[s]]
                for k in range(4):
                    src = (c.xs if k < 2 else c.tmp)[:, s, (k % 2) * P:(k % 2 + 1) * P]
                    ins = nc.tensor.transpose(bank[:, k * P:(k + 1) * P], src, c.ident[:, :])
                ins.then_inc(c.s_tr.sem, 1)
                pe.wait_ge(c.s_xt.sem, t + (xt0 + 1))
                if not early:
                    pe.wait_ge(c.s_out.sem, t + (out0 + 1 - UN))
                for k in range(4):
                    w = c.w[:, k % 2, (k // 2) * D:(k // 2 + 1) * D]
                    nc.tensor.matmul(banks_o[s], c.xt2[:, s, k * P:(k + 1) * P], w, start=k == 0, stop=False)
                nc.tensor.matmul(banks_o[s], c.ones[0:1, :], c.bias[0:1, layer, :], start=False, stop=True
                                 ).then_inc(c.s_lin.sem, 1)

            unrolled(pe, body)
    for s in (c.s_scaled, c.s_tr, c.s_xt, c.s_lin, c.s_out, c.s_dve):
        s.n += NT


def phase_attention_weights(nc, c, m):
    pe0, dve0, act0 = c.s_pe.n, c.s_dve.n, c.s_scaled.n
    w3 = c.acc[:, :, :].rearrange("p t d -> p (t d)")[:, 0:6 * 3 * D].rearrange("p (q n) -> p q n", q=6)
    a_row = c.h[:, 0:3, :].rearrange("p t d -> p (t d)")
    rest = R - P
    phase_load(nc, c, [(w3, c.ins["L3_gnn_W3"].rearrange("(q p) n -> p q n", p=P)),
                       (a_row, c.ins["L3_gnn_a"].rearrange("n o -> o n").to_broadcast([P, 3 * D])),
                       (c.w[:, :, 0:D], halves(c.ins["L3_gnn_weight_neighbor"])),
                       (c.w[:, :, D:2 * D], halves(c.ins["L3_gnn_loop_weight"])),
                       (c.w[:, :, 2 * D:3 * D], halves(c.ins["L3_gnn_evolve_loop_weight"])),
                       (m.rel[:, 0, :], c.ins["L3_gnn_rel_emb"][0:P, :]),
                       (m.rel[0:rest, 1, :], c.ins["L3_gnn_rel_emb"][P:R, :])])
    with nc.Block() as block:

        @block.vector
        def _(dve):
            v = nc.vector
            ch = Chain(dve, c.s_dve)
            for q in range(6):
                ch.inc(v.tensor_tensor_reduce(out=c.h[:, 4:7, :].rearrange("p t d -> p (t d)"), in0=w3[:, q, :],
                                              in1=a_row, scale=1.0, scalar=0.0, op0=ALU.mult, op1=ALU.add,
                                              accum_out=m.wv[:, q:q + 1]))
                ch.wait()
            for q in range(4):
                ch.inc(v.tensor_copy(m.wide[:, q, :], m.wv[:, 2 + q:3 + q].to_broadcast([P, P])))

        @block.tensor
        def _(pe):
            for k in range(2):
                nc.tensor.transpose(c.psum[0][:, k * D:k * D + P], m.rel[:, 0, k * P:(k + 1) * P], c.ident[:, :])
                ins = nc.tensor.transpose(c.psum[0][:, k * D + P:k * D + R], m.rel[0:rest, 1, k * P:(k + 1) * P],
                                          c.ident[0:rest, 0:rest])
            ins.then_inc(c.s_pe.sem, 1)

        @block.scalar
        def _(act):
            act.wait_ge(c.s_pe.sem, pe0 + 1)
            for k in range(2):
                ins = nc.scalar.copy(m.rel_t[:, k, :], c.psum[0][:, k * D:k * D + R])
            ins.then_inc(c.s_scaled.sem, 1)
    c.s_pe.n += 1
    c.s_scaled.n += 1
    with nc.Block() as block:

        @block.tensor
        def _(pe):
            for k in range(2):
                nc.tensor.matmul(c.psum[1][:, 0:R], m.wide[:, 2 + k, :], m.rel_t[:, k, :], start=k == 0, stop=k == 1)
            for k in range(2):
                nc.tensor.matmul(c.psum[2][:, 0:D], m.rel_t[:, k, 0:P], c.w[:, k, 0:D], start=k == 0, stop=k == 1)
            for k in range(2):
                ins = nc.tensor.matmul(c.psum[3][0:rest, 0:D], m.rel_t[:, k, P:R], c.w[:, k, 0:D],
                                       start=k == 0, stop=k == 1)
            ins.then_inc(c.s_pe.sem, 1)

        @block.vector
        def _(dve):
            v = nc.vector
            ch = Chain(dve, c.s_dve)
            dve.wait_ge(c.s_pe.sem, c.s_pe.n + 1)
            ch.inc(v.tensor_copy(m.rel_score[:, :], c.psum[1][:, 0:R]))
            ch.inc(v.tensor_copy(m.rel_w[:, 0, :], c.psum[2][:, 0:D]))
            ch.inc(v.tensor_copy(m.rel_w[0:rest, 1, :], c.psum[3][0:rest, 0:D]))
            ch.inc(v.tensor_scalar(m.neg_et[:, :], c.col_et[:, :], -1.0, None, ALU.mult))
            ch.inc(v.tensor_copy(c.accd, c.x[:, :, :]))
            ch.inc(v.memset(c.acc[:, :, D:D + 4], 0.0))
    c.s_pe.n += 1


def phase_node_scores(nc, c, m):
    sc0, tr0, xt0, lin0, out0 = (s.n for s in (c.s_scaled, c.s_tr, c.s_xt, c.s_lin, c.s_out))
    banks_t = [c.psum[s // 2][:, (s % 2) * D:(s % 2 + 1) * D] for s in range(UN)]
    with nc.Block() as block:

        @block.scalar
        def _(act):
            def body(t, s, early):
                if not early:
                    act.wait_ge(c.s_tr.sem, t + (tr0 + 1 - UN))
                nc.scalar.copy(c.xs[:, s, :], tile_of(c.x, t)).then_inc(c.s_scaled.sem, 1)
                act.wait_ge(c.s_tr.sem, t + (tr0 + 1))
                if not early:
                    act.wait_ge(c.s_lin.sem, t + (lin0 + 1 - UN))
                nc.scalar.copy(c.xt[:, s, :], banks_t[s]).then_inc(c.s_xt.sem, 1)

            unrolled(act, body)

        @block.tensor
        def _(pe):
            def body(t, s, early):
                pe.wait_ge(c.s_scaled.sem, t + (sc0 + 1))
                if not early:
                    pe.wait_ge(c.s_xt.sem, t + (xt0 + 1 - UN))
                for k in range(2):
                    ins = nc.tensor.transpose(banks_t[s][:, k * P:(k + 1) * P], c.xs[:, s, k * P:(k + 1) * P],
                                              c.ident[:, :])
                ins.then_inc(c.s_tr.sem, 1)
                pe.wait_ge(c.s_xt.sem, t + (xt0 + 1))
                if not early:
                    pe.wait_ge(c.s_out.sem, t + (out0 + 1 - UN))
                for k in range(2):
                    nc.tensor.matmul(c.psum[3 + s][:, P:P + 1], c.xt[:, s, k * P:(k + 1) * P], m.wv[:, k:k + 1],
                                     start=k == 0, stop=k == 1)
                for k in range(2):
                    ins = nc.tensor.matmul(c.psum[3 + s][:, 0:P], m.wide[:, k, :], c.xt[:, s, k * P:(k + 1) * P],
                                           start=k == 0, stop=k == 1)
                ins.then_inc(c.s_lin.sem, 1)

            unrolled(pe, body)

        @block.vector
        def _(dve):
            def body(t, s, early):
                dve.wait_ge(c.s_lin.sem, t + (lin0 + 1))
                nc.vector.tensor_copy(m.dst_score[:, bass.ds(t * P, P)], c.psum[3 + s][:, 0:P])
                nc.vector.tensor_copy(c.acc[:, bass.ds(t, 1), D:D + 1].rearrange("p o d -> p (o d)"),
                                      c.psum[3 + s][:, P:P + 1]).then_inc(c.s_out.sem, 1)

            unrolled(dve, body)
    for s in (c.s_scaled, c.s_tr, c.s_xt, c.s_lin, c.s_out):
        s.n += NT


def phase_attention_edges(nc, c, m):
    st0, sel0, mm0, add0, al0, sco0, rel0 = (s.n for s in (c.s_stage, c.s_sel, c.s_mm, c.s_add, c.s_alpha,
                                                         c.s_score, c.s_rel))
    gat0 = [s.n for s in c.s_gat]
    dve0 = c.s_dve.n
    with nc.Block() as block:

        @block.gpsimd
        def _(pool):
            def copy_indices(group, slot):
                nc.gpsimd.tensor_copy(c.stage[:, slot * GRP:(slot + 1) * GRP],
                                      c.col_src[:, bass.ds(group * GRP, GRP)]).then_inc(c.s_stage.sem, 1)

            def gather(slot, ring):
                for j in range(GRP):
                    nc.gpsimd.indirect_dma_start(
                        c.gat[:, ring * GRP + j, :], None, c.ltab,
                        bass.IndirectOffsetOnAxis(c.stage[:, slot * GRP + j:slot * GRP + j + 1], 0)
                    ).then_inc(c.s_gat[ring * GRP + j].sem, 16)

            copy_indices(0, 0)
            copy_indices(1, 1)
            for g in range(4):
                if g >= 2:
                    pool.wait_ge(c.s_mm.sem, mm0 + GRP * (g - 1))
                pool.wait_ge(c.s_stage.sem, st0 + g + 1)
                copy_indices(g + 2, (g + 2) % 4)
                gather(g % 4, g % 2)
            with pool.Fori(1, NG // 4) as it:
                for s in range(4):
                    pool.wait_ge(c.s_mm.sem, it * (4 * GRP) + (mm0 + GRP * (s - 1)))
                    pool.wait_ge(c.s_stage.sem, it * 4 + (st0 + s + 1))
                    copy_indices(it * 4 + (s + 2), (s + 2) % 4)
                    gather(s, s % 2)

        @block.scalar
        def _(act):
            def group(g, ring, first):
                for j in range(GRP):
                    if first and ring == 0 and j == 0:
                        pass
                    k = ring * GRP + j
                    act.wait_ge(c.s_rel.sem, g * (2 * GRP) + (rel0 + 2 * j)) if not (first and k == 0) else None
                    if not first:
                        act.wait_ge(c.s_mm.sem, g * GRP + (mm0 + j + 1 - 2 * GRP))
                    nc.scalar.activation(m.rel_hot[:, k, :], m.lane_r[:, :], ACT.Square,
                                         bias=m.neg_et[:, bass.ds(g * GRP + j, 1)]).then_inc(c.s_rel.sem, 1)
                    act.wait_ge(c.s_rel.sem, g * (2 * GRP) + (rel0 + 2 * j + 1))
                    nc.scalar.activation(m.rel_hot[:, k, :], m.rel_hot[:, k, :], ACT.Relu, bias=c.ones[:, 0:1],
                                         scale=-1.0).then_inc(c.s_rel.sem, 1)
                act.wait_ge(c.s_score.sem, g + (sco0 + 1))
                nc.scalar.activation(m.expo[:, ring, :], m.score[:, ring, :], ACT.Exp).then_inc(c.s_alpha.sem, 1)
            for ring in range(2):
                group(ring, ring, True)
            with act.Fori(1, NG // 2) as it:
                for ring in range(2):
                    group(it * 2 + ring, ring, False)

        @block.vector
        def _(dve):
            v = nc.vector

            def group(g, ring, turn):
                base = dve0
                tiles = [dve.value_load(c.tile_row[0:1, bass.ds(g * GRP + j, 1)], min_val=0, max_val=NT - 1)
                         for j in range(GRP)]
                for j in range(GRP):
                    v.scalar_tensor_tensor(m.junk[:, 0:P], c.lane[:, :], c.col_dst[:, bass.ds(g * GRP + j, 1)],
                                           m.dst_score[:, bass.ds(tiles[j] * P, P)], ALU.is_equal, ALU.mult,
                                           accum_out=m.by_dst[:, ring, j:j + 1]).then_inc(c.s_dve.sem, 1)
                    dve.wait_ge(c.s_dve.sem, g * (2 * GRP + 5) + (dve0 + 2 * j + 1))
                    v.scalar_tensor_tensor(m.junk[:, 0:R], m.lane_r[:, :], c.col_et[:, bass.ds(g * GRP + j, 1)],
                                           m.rel_score[:, :], ALU.is_equal, ALU.mult,
                                           accum_out=m.by_rel[:, ring, j:j + 1]).then_inc(c.s_dve.sem, 1)
                    dve.wait_ge(c.s_dve.sem, g * (2 * GRP + 5) + (dve0 + 2 * j + 2))
                for j in range(GRP):
                    dve.wait_ge(c.s_gat[ring * GRP + j].sem, turn * 16 + (gat0[ring * GRP + j] + 16))
                v.tensor_tensor(m.score[:, ring, :], m.by_dst[:, ring, :], m.by_rel[:, ring, :], ALU.add
                                ).then_inc(c.s_dve.sem, 1)
                dve.wait_ge(c.s_dve.sem, g * (2 * GRP + 5) + (dve0 + 2 * GRP + 1))
                v.tensor_tensor(m.score[:, ring, :], m.score[:, ring, :], c.gat[:, ring * GRP:(ring + 1) * GRP, D],
                                ALU.add).then_inc(c.s_dve.sem, 1)
                dve.wait_ge(c.s_dve.sem, g * (2 * GRP + 5) + (dve0 + 2 * GRP + 2))
                v.tensor_scalar(m.leak[:, ring, :], m.score[:, ring, :], 0.01, None, ALU.mult).then_inc(c.s_dve.sem, 1)
                dve.wait_ge(c.s_dve.sem, g * (2 * GRP + 5) + (dve0 + 2 * GRP + 3))
                v.tensor_tensor(m.score[:, ring, :], m.score[:, ring, :], m.leak[:, ring, :], ALU.max
                                ).then_inc(c.s_score.sem, 1)
                dve.wait_ge(c.s_alpha.sem, g + (al0 + 1))
                v.reciprocal(m.alpha[:, ring, :], m.expo[:, ring, :]).then_inc(c.s_dve.sem, 1)
                dve.wait_ge(c.s_dve.sem, g * (2 * GRP + 5) + (dve0 + 2 * GRP + 4))
                v.tensor_tensor(m.alpha[:, ring, :], m.alpha[:, ring, :], m.expo[:, ring, :], ALU.mult
                                ).then_inc(c.s_dve.sem, 1)
                dve.wait_ge(c.s_dve.sem, g * (2 * GRP + 5) + (dve0 + 2 * GRP + 5))
                for j in range(GRP):
                    v.tensor_scalar(c.sel[:, ring * GRP + j, :], c.lane[:, :], c.col_dst[:, bass.ds(g * GRP + j, 1)],
                                    m.alpha[:, ring, j:j + 1], ALU.is_equal, ALU.mult).then_inc(c.s_sel.sem, 1)
                for j in range(GRP):
                    dve.wait_ge(c.s_mm.sem, g * GRP + (mm0 + j + 1))
                    if not (isinstance(g, int) and g == 0 and j == 0):
                        dve.wait_ge(c.s_add.sem, g * GRP + (add0 + j))
                    into = c.acc[:, bass.ds(tiles[j], 1), :].rearrange("p o d -> p (o d)")
                    v.tensor_tensor(into, into, c.psum[j][:, 0:D + R], ALU.add).then_inc(c.s_add.sem, 1)

            with dve.Fori(0, NG // 2) as it:
                for ring in range(2):
                    group(it * 2 + ring, ring, it)

        @block.tensor
        def _(pe):
            def group(g, ring, turn, first):
                pe.wait_ge(c.s_sel.sem, g * GRP + (sel0 + GRP))
                for j in range(GRP):
                    k = ring * GRP + j
                    pe.wait_ge(c.s_gat[k].sem, turn * 16 + (gat0[k] + 16))
                    if not first:
                        pe.wait_ge(c.s_add.sem, g * GRP + (add0 + j + 1 - GRP))
                    nc.tensor.matmul(c.psum[j][:, 0:D], c.sel[:, k, :], c.gat[:, k, 0:D], start=True, stop=True)
                    pe.wait_ge(c.s_rel.sem, g * (2 * GRP) + (rel0 + 2 * j + 2))
                    nc.tensor.matmul(c.psum[j][:, D:D + R], c.sel[:, k, :], m.rel_hot[:, k, :], start=True, stop=True
                                     ).then_inc(c.s_mm.sem, 1)
            group(0, 0, 0, True)
            group(1, 1, 0, False)
            with pe.Fori(1, NG // 2) as it:
                for ring in range(2):
                    group(it * 2 + ring, ring, it, False)
    c.s_stage.n += NG + 2
    c.s_sel.n += NI
    c.s_mm.n += NI
    c.s_add.n += NI
    c.s_alpha.n += NG
    c.s_score.n += NG
    c.s_rel.n += 2 * NI
    c.s_dve.n += NG * (2 * GRP + 5)
    for s in c.s_gat:
        s.n += 16 * NG // 2


def phase_attention_linear(nc, c, m):
    sc0, tr0, xt0, lin0, out0, dve0 = (s.n for s in (c.s_scaled, c.s_tr, c.s_xt, c.s_lin, c.s_out, c.s_dve))
    rest = R - P
    banks = [(c.psum[0], c.psum[1], c.psum[2], c.psum[3]), (c.psum[4], c.psum[5], c.psum[6], c.psum[7])]
    with nc.Block() as block:

        @block.vector
        def _(dve):
            ch = Chain(dve, c.s_dve)
            v = nc.vector
            ch.step(v.tensor_scalar(m.no_in[:, :], c.has_in[:, :], -1.0, 1.0, ALU.mult, ALU.add))
            first = c.s_dve.n
            for t in range(NT):
                b = banks[t % 2]
                if t >= 2:
                    dve.wait_ge(c.s_tr.sem, tr0 + t - 1)
                dve.wait_ge(c.s_lin.sem, lin0 + t + 1)
                v.tensor_scalar(c.tmp[:, t % 2, :], b[2][:, 0:D], 0.0, None, ALU.max).then_inc(c.s_dve.sem, 1)
                dve.wait_ge(c.s_dve.sem, first + 2 * t + 1)
                v.scalar_tensor_tensor(c.h[:, t, :], b[3][:, 0:D], c.has_in[:, t:t + 1], c.tmp[:, t % 2, :],
                                       ALU.mult, ALU.add).then_inc(c.s_dve.sem, 1)
                dve.wait_ge(c.s_dve.sem, first + 2 * t + 2)
                v.scalar_tensor_tensor(c.h[:, t, :], b[3][:, D:2 * D], m.no_in[:, t:t + 1], c.h[:, t, :],
                                       ALU.mult, ALU.add).then_inc(c.s_out.sem, 1)
            c.s_dve.n += 2 * NT

        @block.scalar
        def _(act):
            for t in range(NT):
                b = banks[t % 2]
                if t >= 2:
                    act.wait_ge(c.s_lin.sem, lin0 + t - 1)
                act.wait_ge(c.s_tr.sem, tr0 + t + 1)
                nc.scalar.copy(m.xt3[:, t % 2, 0:2 * D], b[0][:, :])
                nc.scalar.copy(m.xt3[:, t % 2, 2 * D:3 * D], b[1][:, 0:D]).then_inc(c.s_xt.sem, 1)

        @block.tensor
        def _(pe):
            for t in range(NT):
                b = banks[t % 2]
                if t >= 2:
                    pe.wait_ge(c.s_xt.sem, xt0 + t - 1)
                for k in range(2):
                    nc.tensor.transpose(b[0][:, k * P:(k + 1) * P], c.acc[:, t, k * P:(k + 1) * P], c.ident[:, :])
                nc.tensor.transpose(b[0][:, D:D + P], c.acc[:, t, D:D + P], c.ident[:, :])
                nc.tensor.transpose(b[0][0:rest, D + P:2 * D], c.acc[:, t, D + P:D + R], c.ident[:, :])
                for k in range(2):
                    ins = nc.tensor.transpose(b[1][:, k * P:(k + 1) * P], c.x[:, t, k * P:(k + 1) * P], c.ident[:, :])
                ins.then_inc(c.s_tr.sem, 1)
                pe.wait_ge(c.s_xt.sem, xt0 + t + 1)
                if t >= 2:
                    pe.wait_ge(c.s_out.sem, out0 + t - 1)
                xt = m.xt3[:, t % 2, :]
                for k in range(2):
                    nc.tensor.matmul(b[2][:, 0:D], xt[:, k * P:(k + 1) * P], c.w[:, k, 0:D], start=k == 0, stop=False)
                nc.tensor.matmul(b[2][:, 0:D], xt[:, D:D + P], m.rel_w[:, 0, :], start=False, stop=False)
                nc.tensor.matmul(b[2][:, 0:D], xt[0:rest, D + P:2 * D], m.rel_w[0:rest, 1, :], start=False, stop=True)
                for k in range(2):
                    ins = nc.tensor.matmul(b[3][:, :], xt[:, 2 * D + k * P:2 * D + (k + 1) * P], c.w[:, k, D:3 * D],
                                           start=k == 0, stop=k == 1)
                ins.then_inc(c.s_lin.sem, 1)
    for s in (c.s_tr, c.s_xt, c.s_lin, c.s_out):
        s.n += NT


def layer_convolutions(nc, c):
    ins = c.ins
    for k in range(3):
        loads = [(c.w[:, :, 0:D], halves(ins[f"L0_gnn_W{k + 1}"]))]
        if k == 0:
            loads += [(c.bias[:, j, :], row_of(ins[f"L0_gnn_b{j + 1}"])) for j in range(3)]
        phase_load(nc, c, loads)
        phase_gcn_linear(nc, c, c.x, k)
        phase_edges(nc, c, c.tab, c.col_src)
    phase_norm(nc, c, c.dinv, c.bias[:, 2, :])


def layer_relations(nc, c):
    ins = c.ins
    phase_load(nc, c, [(c.w[:, k, :].rearrange("p (r n) -> p r n", r=NREL),
                        ins["L1_gnn_weight"][:, k * P:(k + 1) * P, :].rearrange("r p n -> p r n")) for k in range(2)] +
               [(c.bias[:, 0, :], row_of(ins["L1_gnn_gamma"])), (c.bias[:, 1, :], row_of(ins["L1_gnn_beta"]))])
    phase_relation_table(nc, c)
    phase_zero(nc, c, D)
    phase_edges(nc, c, c.rtab, c.col_src8)
    phase_batch_norm(nc, c)
    phase_norm(nc, c, None, None)


def layer_sage(nc, c):
    ins = c.ins
    for k in range(3):
        source = c.x if k == 0 else c.h
        loads = [(c.w[:, :, 0:D], halves(ins[f"L2_gnn_W{k}_self"])), (c.w[:, :, D:2 * D], halves(ins[f"L2_gnn_W{k}_neigh"]))]
        if k == 0:
            loads += [(c.bias[:, j, :], row_of(ins[f"L2_gnn_b{j}"])) for j in range(3)]
        phase_load(nc, c, loads)
        phase_to_table(nc, c, source[:, :, :], c.tab, D)
        phase_edges(nc, c, c.tab, c.col_src)
        phase_sage_linear(nc, c, source, k)
    phase_norm(nc, c, None, None)


def layer_attention(nc, c):
    with ExitStack() as ctx:
        m = Core()

        def sb(name, shape, dt=F32):
            return ctx.enter_context(nc.sbuf_tensor(name, shape, dt))

        m.rel = sb("m_rel", [P, 2, D])
        m.rel_t = sb("m_rel_t", [P, 2, R])
        m.rel_w = sb("m_rel_w", [P, 2, D])
        m.wv = sb("m_wv", [P, 6])
        m.wide = sb("m_wide", [P, 4, P])
        m.rel_score = sb("m_rel_score", [P, R])
        flat = c.h[:, :, :].rearrange("p t d -> p (t d)")
        m.dst_score = flat[:, 0:NT * P]
        m.neg_et = sb("m_neg_et", [P, NIP])
        m.lane_r = c.lane_r
        m.rel_hot = flat[:, NT * P:NT * P + 2 * GRP * R].rearrange("p (s r) -> p s r", r=R)
        m.junk = sb("m_junk", [P, R])
        m.by_dst, m.by_rel, m.score, m.leak, m.expo, m.alpha = (
            sb("m_" + name, [P, 2, GRP]) for name in ("by_dst", "by_rel", "score", "leak", "expo", "alpha"))
        m.no_in = sb("m_no_in", [P, NT])
        m.xt3 = c.w[:, :, 4 * D:7 * D]
        phase_attention_weights(nc, c, m)
        phase_node_scores(nc, c, m)
        phase_to_table(nc, c, c.acc[:, :, 0:D + 4], c.ltab, D + R)
        phase_attention_edges(nc, c, m)
        phase_attention_linear(nc, c, m)
        phase_norm(nc, c, None, None)


def row_of(v):
    return v.rearrange("(o d) -> o d", o=1).to_broadcast([P, D])


def build(nc, ins, out, stage=3):
    c = Core()
    c.ins = ins
    with ExitStack() as ctx:
        allocate(nc, ctx, c)
        phase_start(nc, c)
        prepare(nc, c)
        layer_convolutions(nc, c)
        if stage >= 1:
            layer_relations(nc, c)
        if stage >= 2:
            layer_sage(nc, c)
        if stage >= 3:
            layer_attention(nc, c)
        phase_store(nc, c, out)


NAMES = {"x": "x", "src": "src", "dst": "dst", "et200": "edge_type_200", "et8": "edge_type_8"}


def kernel(**inputs):
    import numpy as _np
    import concourse.bacc as _bacc
    from concourse import mybir as _mybir
    from concourse.bass_utils import run_bass_kernel_spmd as _run

    nc = _bacc.Bacc("TRN2", target_bir_lowering=False, num_devices=1)
    short = {v: k for k, v in NAMES.items()}
    arrays, args = {}, {}
    for name in inputs:
        a = _np.ascontiguousarray(inputs[name])
        arrays[f"in_{name}"] = a
        args[short.get(name, name)] = nc.dram_tensor(f"in_{name}", a.shape, _mybir.dt.from_np(a.dtype),
                                                     kind="ExternalInput").ap()
    out = nc.dram_tensor("out_0", (N, D), _mybir.dt.float32, kind="ExternalOutput").ap()
    build(nc, args, out)
    r = _run(nc, [arrays], core_ids=[0])
    return r.results[0]["out_0"]
```

```python
import concourse.bass as bass
from concourse import mybir
from contextlib import ExitStack

F32 = mybir.dt.float32
BF16 = mybir.dt.bfloat16
F16 = mybir.dt.float16
I16 = mybir.dt.int16
I32 = mybir.dt.int32
ALU = mybir.AluOpType
ACT = mybir.ActivationFunctionType
AX = mybir.AxisListType

P = 128
N = 3125
D = 256
E = 50000
NT = -(-N // P)
LAST = N - (NT - 1) * P
NC = -(-E // P)
EP = NC * P
NREL = 8
R = 200
WHOLE = 2048
EPS = 1e-5
PAD_DST = 8000
NI = NC + NT
NIP = 512
GRP = 8
NG = NI // GRP
DEEP = 4
UN = 5
assert NG % DEEP == 0 and NT % UN == 0


class Count:

    def __init__(self, ctx, nc, name):
        self.sem = ctx.enter_context(nc.semaphore(name))
        self.n = 0


class Chain:

    def __init__(self, eng, count):
        self.eng, self.count = eng, count

    def inc(self, ins, times=1):
        ins.then_inc(self.count.sem, 1)
        self.count.n += times

    def wait(self):
        self.eng.wait_ge(self.count.sem, self.count.n)

    def step(self, ins):
        self.inc(ins)
        self.wait()


class Core:
    pass


def edge_memory(nc, ctx, c, part):
    def sb(name, shape, dt=F32):
        return ctx.enter_context(nc.sbuf_tensor(f"{name}_{part}", shape, dt))

    c.x = sb("x_res", [P, NT, D])
    c.h = sb("h_cur", [P, NT, D])
    c.acc = sb("acc", [P, NT, D + R])
    c.accd = c.acc[:, :, 0:D]
    c.col_dst = sb("col_dst", [P, NIP])
    c.col_src = sb("col_src", [P, NIP], I32)
    c.col_src8 = sb("col_src8", [P, NIP], I32)
    c.col_et = sb("col_et", [P, NIP])
    c.gat = sb("gat", [P, DEEP * GRP, D + 4])
    c.stage = sb("stage", [P, DEEP * GRP], I32)
    c.sel = sb("sel", [P, 2 * GRP, P])
    c.xs = sb("xs", [P, UN, D])
    c.xt = sb("xt", [P, UN, D])
    c.tmp = sb("tmp", [P, UN, D])
    c.w = sb("w", [P, 2, NREL * D])
    c.bias = sb("bias", [P, 3, D])
    c.idle = sb("idle", [P, 1])
    c.node_no = sb("node_no", [P, P])
    c.lane_r = sb("lane_r", [P, R])
    c.valid = sb("valid", [P, P])
    c.mean = sb("mean", [P, D])
    c.gain = sb("gain", [P, D])
    c.stats = sb("stats", [P, NT, 6])
    c.mv = sb("mv", [P, NT, 2])
    c.var = sb("var", [P, NT])
    c.rstd = sb("rstd", [P, NT])
    c.root = sb("root", [P, 2 * D])
    c.xt2 = sb("xt2", [P, UN, 2 * D])


def allocate(nc, ctx, c):
    def sb(name, shape, dt=F32):
        return ctx.enter_context(nc.sbuf_tensor(name, shape, dt))

    def sem(name):
        return Count(ctx, nc, name)

    c.deg = sb("deg", [P, NT])
    c.dinv = sb("dinv", [P, NT])
    c.ideg = sb("ideg", [P, NT])
    c.has_in = sb("has_in", [P, NT])
    c.ends = sb("ends", [1, NT], I32)
    c.words = sb("words", [1, NIP // GRP], I32)
    c.wv = sb("score_weights", [P, 6])
    c.amax = sb("amax", [P, NT])
    c.ident = sb("ident", [P, P])
    c.ones = sb("ones", [P, P])
    c.lane = sb("lane", [P, P])
    c.heavy = sb("heavy", [1, 1], I32)
    c.minus16 = sb("minus16", [P, P], F16)
    c.ident16 = sb("ident16", [P, P], F16)
    c.psum = [ctx.enter_context(nc.psum_tensor(f"bank{k}", [P, 512], F32)) for k in range(8)]

    c.s_load = sem("loaded")
    c.s_dve = sem("dve_chain")
    c.s_pool = sem("pool_chain")
    c.s_pe = sem("pe_chain")
    c.s_store = sem("stored")
    c.s_gat = [sem(f"gathered{k}") for k in range(DEEP * GRP)]
    c.s_stage = sem("indices_staged")
    c.s_sel = sem("onehots_ready")
    c.s_mm = sem("edge_products_done")
    c.s_add = sem("edge_sums_added")
    c.s_scaled = sem("tile_scaled")
    c.s_tr = sem("tile_transposed")
    c.s_xt = sem("tile_xt_ready")
    c.s_lin = sem("tile_product_done")
    c.s_out = sem("tile_out_ready")

    c.s_odd = sem("odd_banks_out")
    c.s_slot = [sem(f"slot_stored{k}") for k in range(UN)]
    c.s_cols = sem("columns_staged")
    c.s_by = sem("scores_read_off")
    c.s_alpha = sem("alpha_ready")
    c.s_score = sem("scores_ready")
    c.s_rel = sem("relation_steps")

    c.s_hot = sem("source_onehots_ready")
    c.s_visit = sem("visits_counted")
    c.s_taken = sem("banks_taken")
    c.s_agg = sem("tile_aggregated")
    c.s_half = sem("tile_high_part")
    c.s_low = sem("tile_low_part")
    c.s_post = sem("tile_sum_ready")
    c.s_row = [sem(f"tile_loaded{k}") for k in range(2)]
    c.s_sent = [sem(f"tile_sent{k}") for k in range(2)]
    c.s_split = sem("groups_split")
    c.s_keep = sem("counts_kept")
    c.s_back = [sem(f"counts_loaded{k}") for k in range(NT // UN)]
    c.s_round = sem("counts_rounded")
    c.s_less = sem("rest_left_in_bank")
    c.s_rest_kept = sem("rest_kept")
    c.s_rest = sem("rest_loaded")
    c.s_rest_used = sem("rest_used")

    c.planes = nc.dram_tensor("visit_planes", [6, P, NIP], F32, kind="Internal").ap()
    c.counts = nc.dram_tensor("count_matrix", [NT // UN, P, NT, UN * P], F16, kind="Internal").ap()
    c.rests = nc.dram_tensor("count_rests", [NT, P, NT * P], F16, kind="Internal").ap()
    c.xbuf = nc.dram_tensor("layer_input", [NT * P, D], F32, kind="Internal").ap()
    c.hbuf = [nc.dram_tensor(f"hidden{k}", [NT * P, D], F32, kind="Internal").ap() for k in range(2)]
    c.rec = nc.dram_tensor("edge_records", [EP, 4], I32, kind="Internal").ap()
    c.rtab = nc.dram_tensor("relation_table", [NT * P * NREL, D], F32, kind="Internal").ap()
    c.ltab = nc.dram_tensor("scored_table", [NT * P, D + 4], F32, kind="Internal").ap()
    c.tab = nc.dram_tensor("row_table", [NT * P, D], F32, kind="Internal").ap()


def phase_constants_and_planes(nc, c, p):
    load0, dve0, pool0 = c.s_load.n, c.s_dve.n, c.s_pool.n
    planes = [("src", p.src), ("dst", p.dst), ("et8", p.et8), ("et200", p.et200)]
    whole = E // NC
    with nc.Block() as block:

        @block.gpsimd
        def _(pool):
            ch = Chain(pool, c.s_pool)
            for k, (name, plane) in enumerate(planes):
                ch.inc(nc.gpsimd.memset(plane[:, :], PAD_DST if name == "dst" else 0))
            ch.inc(nc.gpsimd.iota(p.edge_no[:, :], [[1, NC]], base=0, channel_multiplier=NC,
                                  allow_small_or_imprecise_dtypes=True))
            ch.inc(nc.gpsimd.iota(c.lane[:, :], [[1, P]], base=0, channel_multiplier=0,
                                  allow_small_or_imprecise_dtypes=True))
            ch.inc(nc.gpsimd.iota(p.part_no[:, :], [[1, 1]], base=0, channel_multiplier=1,
                                  allow_small_or_imprecise_dtypes=True))
            ch.inc(nc.gpsimd.memset(c.ones[:, :], 1.0))
            ch.inc(nc.gpsimd.memset(p.zero[:, :], 0.0))

        @block.sync
        def _(sp):
            sp.wait_ge(c.s_pool.sem, pool0 + 4)
            for k, (name, plane) in enumerate(planes):
                src = c.ins[name]
                sp.dma_start(plane[0:whole, :], src[0:whole * NC].rearrange("(p j) -> p j", j=NC)
                             ).then_inc(c.s_load.sem, 16)
                sp.dma_start(plane[whole:whole + 1, 0:E - whole * NC],
                             src[whole * NC:E].rearrange("(o j) -> o j", o=1)).then_inc(c.s_load.sem, 16)
            sp.dma_start(c.x[:, 0:NT - 1, :], c.ins["x"][0:(NT - 1) * P, :].rearrange("(t p) d -> p t d", p=P)
                         ).then_inc(c.s_load.sem, 16)
            sp.dma_start(c.x[0:LAST, NT - 1, :], c.ins["x"][(NT - 1) * P:N, :]).then_inc(c.s_load.sem, 16)

        @block.vector
        def _(dve):
            ch = Chain(dve, c.s_dve)
            v = nc.vector
            dve.wait_ge(c.s_pool.sem, pool0 + 9)
            ch.inc(v.tensor_scalar(c.ident[:, :], c.lane[:, :], p.part_no[:, 0:1], None, ALU.is_equal))
            ch.inc(v.tensor_scalar(p.lower[:, :], c.lane[:, :], p.part_no[:, 0:1], None, ALU.is_gt))
            dve.wait_ge(c.s_load.sem, load0 + 160)
            ch.step(v.tensor_single_scalar(p.hi_i[:, :], p.dst[:, :], 7, ALU.arith_shift_right))
            ch.inc(v.tensor_copy(p.lane_b[:, :], c.lane[:, :]))
            ch.step(v.tensor_scalar(p.hi[:, :], p.hi_i[:, :], float(NT), None, ALU.min))
            ch.step(v.tensor_tensor(p.inb[:, :, :], p.hi[:, :].unsqueeze(1).broadcast_to([P, NT + 1, NC]),
                                    p.lane_b[:, 0:NT + 1].unsqueeze(2).broadcast_to([P, NT + 1, NC]), ALU.is_equal))
            flat = p.inb[:, :, :].rearrange("p t j -> p (t j)")
            ch.step(v.tensor_tensor_scan(p.run[:, :, :].rearrange("p t j -> p (t j)"),
                                         p.zero[:, 0:1].broadcast_to([P, (NT + 1) * NC]), flat, 0.0,
                                         ALU.add, ALU.add))
            ch.inc(v.memset(p.before[:, 0:1], 0.0))
            ch.step(v.tensor_copy(p.before[:, 1:NT + 2], p.run[:, :, NC - 1]))
            ch.step(v.tensor_tensor(p.cnt[:, :], p.before[:, 1:NT + 2], p.before[:, 0:NT + 1], ALU.subtract))

        @block.tensor
        def _(pe):
            pe.wait_ge(c.s_dve.sem, c.s_dve.n)
            nc.tensor.matmul(c.psum[0][:, 0:NT + 1], p.lower[:, :], p.cnt[:, :], start=True, stop=True)
            nc.tensor.matmul(c.psum[1][:, 0:NT + 1], c.ones[:, :], p.cnt[:, :], start=True, stop=True
                             ).then_inc(c.s_pe.sem, 1)
    c.s_pool.n = pool0 + 9
    c.s_load.n = load0 + 160
    c.s_pe.n += 1

    with nc.Block() as block:
        pe1 = c.s_pe.n

        @block.vector
        def _(dve):
            ch = Chain(dve, c.s_dve)
            v = nc.vector
            nb = NT + 1
            ch.inc(v.memset(p.base[:, 0:1], 0.0))
            ch.step(v.tensor_tensor_scan(p.base[:, 1:nb + 1], p.zero[:, 0:1].broadcast_to([P, nb]),
                                         c.psum[1][:, 0:nb], 0.0, ALU.add, ALU.add))
            ch.step(v.tensor_tensor(p.corr[:, :], p.base[:, 0:nb], c.psum[0][:, 0:nb], ALU.add))
            ch.step(v.tensor_tensor(p.corr[:, :], p.corr[:, :], p.before[:, 0:nb], ALU.subtract))
            ch.step(v.tensor_scalar(p.corr[:, :], p.corr[:, :], -1.0, None, ALU.add))
            ch.step(v.tensor_tensor(p.run[:, :, :], p.run[:, :, :],
                                    p.corr[:, :].unsqueeze(2).broadcast_to([P, nb, NC]), ALU.add))
            ch.step(v.tensor_tensor(p.run[:, :, :], p.run[:, :, :], p.inb[:, :, :], ALU.mult))
            ch.step(v.tensor_reduce(p.place[:, :], p.run[:, :, :].rearrange("p t j -> p j t"), AX.X, ALU.add))
            ch.inc(v.tensor_copy(p.place_i[:, :], p.place[:, :]))
            for k, plane in enumerate((p.src, p.dst, p.et8, p.et200)):
                ch.inc(v.tensor_copy(p.rec_sb[:, :, k], plane[:, :]))
            ch.step(v.tensor_tensor(p.off[:, :], p.place[:, :], p.edge_no[:, :], ALU.not_equal))
            ch.step(v.tensor_reduce(p.moved[:, 0:1], p.off[:, :], AX.X, ALU.add))

        @block.tensor
        def _(pe):
            pe.wait_ge(c.s_dve.sem, c.s_dve.n)
            nc.tensor.matmul(c.psum[2][:, 0:1], c.ones[:, :], p.moved[:, 0:1], start=True, stop=True
                             ).then_inc(c.s_pe.sem, 1)
    c.s_pe.n += 1

    with nc.Block() as block:
        dve1, pool1 = c.s_dve.n, c.s_pool.n

        @block.vector
        def _(dve):
            ch = Chain(dve, c.s_dve)
            ch.step(nc.vector.tensor_scalar(p.flag[:, 0:1], c.psum[2][:, 0:1], 1.0, None, ALU.min))

        @block.gpsimd
        def _(pool):
            rec_out = c.rec.rearrange("(p j) k -> p (j k)", j=NC)
            pool.wait_ge(c.s_dve.sem, dve1 + 1)
            flag = pool.value_load(p.flag[0:1, 0:1], min_val=0, max_val=1)
            cond = pool.If(flag == 0)
            with cond:
                pool.dma_start(rec_out, p.rec_sb[:, :, :].rearrange("p j k -> p (j k)")
                               ).then_inc(c.s_copied.sem, 16)
                pool.wait_ge(c.s_copied.sem, 16)
            with pool.Else():
                with pool.Fori(0, NC) as j:
                    nc.gpsimd.tensor_copy(p.one_place[:, 0:1], p.place_i[:, bass.ds(j, 1)])
                    nc.gpsimd.tensor_copy(p.one_rec[:, :], p.rec_sb[:, bass.ds(j, 1), :]
                                          .rearrange("p o k -> p (o k)")).then_inc(c.s_rec.sem, 1)
                    pool.wait_ge(c.s_rec.sem, j + 1)
                    nc.gpsimd.tensor_tensor(p.spare[:, 0:1], p.place_i[:, 0:1], p.place_i[:, 0:1], ALU.add)
                    nc.gpsimd.indirect_dma_start(c.rec, bass.IndirectOffsetOnAxis(p.one_place[:, 0:1], 0),
                                                 p.one_rec[:, :], None).then_inc(c.s_scat.sem, 16)
                    pool.wait_ge(c.s_scat.sem, j * 16 + 16)


def phase_visits(nc, c, p):
    NQ = NIP // P
    NLO = 17
    assert NC % NLO == 0
    load0, dve0, pool0, pe0 = c.s_load.n, c.s_dve.n, c.s_pool.n, c.s_pe.n
    tail = NC - (NQ - 1) * P
    with nc.Block() as block:

        @block.gpsimd
        def _(pool):
            ch = Chain(pool, c.s_pool)
            ch.inc(nc.gpsimd.memset(p.last_dst[:, :], 0))
            ch.inc(nc.gpsimd.iota(p.visit_no[:, :], [[1, NIP]], base=0, channel_multiplier=0,
                                  allow_small_or_imprecise_dtypes=True))
            ch.inc(nc.gpsimd.iota(p.chunk_no[:, :], [[P, NQ]], base=0, channel_multiplier=1,
                                  allow_small_or_imprecise_dtypes=True))

        @block.sync
        def _(sp):
            sp.wait_ge(c.s_pool.sem, pool0 + 1)
            ends = c.rec.rearrange("(j e) k -> j (e k)", e=P)
            with nc.allow_non_contiguous_dma(reason="one word per chunk"):
                for q in range(NQ):
                    rows = P if q < NQ - 1 else tail
                    sp.dma_start(p.last_dst[0:rows, q:q + 1], ends[q * P:q * P + rows, 4 * (P - 1) + 1:4 * (P - 1) + 2]
                                 ).then_inc(c.s_load.sem, 16)

        @block.vector
        def _(dve):
            ch = Chain(dve, c.s_dve)
            v = nc.vector
            ch.step(v.tensor_single_scalar(p.hi_i[:, :], p.dst[:, :], P - 1, ALU.bitwise_and))
            ch.step(v.tensor_copy(p.lo[:, :], p.hi_i[:, :]))
            def onehots(g, slot):
                return v.tensor_tensor(p.lo_hot[:, slot, :, :],
                                       p.lo[:, bass.ds(g * NLO, NLO)].unsqueeze(2).broadcast_to([P, NLO, P]),
                                       p.lane_b[:, :].unsqueeze(1).broadcast_to([P, NLO, P]), ALU.is_equal)
            for g in range(3):
                if g >= 2:
                    dve.wait_ge(c.s_pe.sem, pe0 + g - 1)
                onehots(g, g % 2).then_inc(c.s_sel.sem, 1)
            with dve.Fori(1, NC // NLO // 2) as it:
                for s in range(2):
                    dve.wait_ge(c.s_pe.sem, pe0 + it * 2 + s)
                    onehots(it * 2 + 1 + s, (1 + s) % 2).then_inc(c.s_sel.sem, 1)

        @block.tensor
        def _(pe):
            def count(g, slot, first, last):
                for k in range(NLO):
                    ins = nc.tensor.matmul(c.psum[7][:, 0:NT], p.lo_hot[:, slot, k, :],
                                           p.inb[:, 0:NT, bass.ds(g * NLO + k, 1)].rearrange("p t o -> p (t o)"),
                                           start=first and k == 0, stop=last and k == NLO - 1,
                                           skip_group_check=True)
                ins.then_inc(c.s_pe.sem, 1)
            pe.wait_ge(c.s_sel.sem, 1)
            count(0, 0, True, False)
            with pe.Fori(0, NC // NLO // 2) as it:
                for s in range(2):
                    pe.wait_ge(c.s_sel.sem, it * 2 + 2 + s)
                    count(it * 2 + 1 + s, (1 + s) % 2, False, False)
    c.s_load.n += 16 * NQ
    c.s_sel.n += NC // NLO
    c.s_pe.n += NC // NLO

    with nc.Block() as block:

        @block.vector
        def _(dve):
            ch = Chain(dve, c.s_dve)
            v = nc.vector
            dve.wait_ge(c.s_load.sem, c.s_load.n)
            ch.step(v.tensor_single_scalar(p.last_hi[:, :], p.last_dst[:, :], 7, ALU.arith_shift_right))
            ch.inc(v.tensor_scalar(p.past[:, :], p.chunk_no[:, :], float(NC), 1e6, ALU.is_ge, ALU.mult))
            ch.step(v.tensor_scalar(p.leave[:, :], p.last_hi[:, :], float(NT - 1), None, ALU.min))
            ch.step(v.tensor_tensor(p.leave[:, :], p.leave[:, :], p.chunk_no[:, :], ALU.add))
            ch.step(v.tensor_tensor(p.leave[:, :], p.leave[:, :], p.past[:, :], ALU.add))
            for q in range(NQ):
                ch.inc(v.tensor_scalar(p.gone[:, q, :], p.visit_no[:, :], p.leave[:, q:q + 1], None, ALU.is_gt))
            ch.step(v.tensor_copy(c.deg[:, :], c.psum[7][:, 0:NT]))
            ch.step(v.tensor_scalar(p.over[:, :], c.deg[:, :], float(WHOLE), None, ALU.is_gt))
            ch.inc(v.tensor_reduce(p.many[:, 0:1], p.over[:, :], AX.X, ALU.max))
            ch.inc(v.tensor_scalar(p.deg_loop[:, :], c.deg[:, :], 1.0, None, ALU.add))
            ch.inc(v.tensor_scalar(c.has_in[:, :], c.deg[:, :], 1.0, None, ALU.min))
            ch.step(v.tensor_scalar(c.ideg[:, :], c.deg[:, :], 1.0, None, ALU.max))
            ch.step(v.reciprocal(c.ideg[:, :], c.ideg[:, :]))

        @block.tensor
        def _(pe):
            pe.wait_ge(c.s_dve.sem, c.s_dve.n)
            for q in range(NQ):
                nc.tensor.matmul(c.psum[0][:, :], c.ones[:, :], p.gone[:, q, :],
                                 start=q == 0, stop=q == NQ - 1)
            ins = nc.tensor.matmul(c.psum[6][:, 0:1], c.ones[:, :], p.many[:, 0:1], start=True, stop=True)
            ins.then_inc(c.s_pe.sem, 1)
    c.s_pe.n += 1

    with nc.Block() as block:

        @block.vector
        def _(dve):
            ch = Chain(dve, c.s_dve)
            v = nc.vector
            ch.inc(v.tensor_scalar(c.heavy[0:1, 0:1], c.psum[6][0:1, 0:1], 1.0, None, ALU.min))
            ch.step(v.tensor_scalar(p.chunk_row[:, :], c.psum[0][:, :], float(NC - 1), None, ALU.min))
            ch.step(v.tensor_tensor(p.tile_f[:, :], p.visit_no[:, :], p.chunk_row[:, :], ALU.subtract))

        @block.tensor
        def _(pe):
            pe.wait_ge(c.s_dve.sem, c.s_dve.n)
            for q in range(NQ):
                ins = nc.tensor.transpose(c.psum[1][:, q * P:(q + 1) * P], p.chunk_row[:, q * P:(q + 1) * P],
                                          c.ident[:, :])
            ins.then_inc(c.s_pe.sem, 1)
    c.s_pe.n += 1

    with nc.Block() as block:
        dve1, load1 = c.s_dve.n, c.s_load.n

        @block.vector
        def _(dve):
            ch = Chain(dve, c.s_dve)
            ch.step(nc.vector.tensor_copy(p.chunk_of[:, :], c.psum[1][:, 0:NQ * P:P]))
            dve.wait_ge(c.s_fetch.sem, 16 * NQ)
            for k in range(4):
                ch.inc(nc.vector.tensor_copy(p.fetched_f[:, :, k, :],
                                             p.fetched[:, :, :].rearrange("p q (e k) -> p q e k", k=4)[:, :, :, k]))

        @block.gpsimd
        def _(pool):
            pool.wait_ge(c.s_dve.sem, dve1 + 1)
            rows = c.rec.rearrange("(j e) k -> j (e k)", e=P)
            for q in range(NQ):
                nc.gpsimd.indirect_dma_start(p.fetched[:, q, :], None, rows,
                                             bass.IndirectOffsetOnAxis(p.chunk_of[:, q:q + 1], 0)
                                             ).then_inc(c.s_fetch.sem, 16)

        @block.tensor
        def _(pe):
            pe.wait_ge(c.s_dve.sem, c.s_dve.n)
            for k in range(4):
                for q in range(NQ):
                    ins = nc.tensor.transpose(c.psum[2 + k][:, q * P:(q + 1) * P], p.fetched_f[:, q, k, :],
                                              c.ident[:, :])
            ins.then_inc(c.s_pe.sem, 1)
    c.s_pe.n += 1

    with nc.Block() as block:

        @block.vector
        def _(dve):
            ch = Chain(dve, c.s_dve)
            v = nc.vector
            src, dst, et8, et200 = c.psum[2], c.psum[3], c.psum[4], c.psum[5]
            ch.inc(v.tensor_copy(c.col_src[:, :], src[:, :]))
            ch.inc(v.tensor_copy(c.col_et[:, :], et200[:, :]))
            ch.inc(v.tensor_copy(p.src_f[:, :], src[:, :]))
            ch.inc(v.tensor_copy(p.dst_f[:, :], dst[:, :]))
            ch.step(v.tensor_scalar(p.first_f[:, :], p.tile_f[:, :], float(P), None, ALU.mult))
            ch.inc(v.tensor_tensor(c.col_dst[:, :], p.dst_f[:, :], p.first_f[:, :], ALU.subtract))
            ch.step(v.tensor_scalar(p.src_f[:, :], p.src_f[:, :], float(NREL), None, ALU.mult))
            ch.step(v.tensor_tensor(p.src_f[:, :], p.src_f[:, :], et8[:, :], ALU.add))
            ch.step(v.tensor_copy(c.col_src8[:, :], p.src_f[:, :]))
            ch.inc(v.tensor_copy(p.src_plain[:, :], src[:, :]))
            ch.inc(v.tensor_copy(c.ident16[:, :], c.ident[:, :]))
            ch.inc(v.tensor_scalar(c.minus16[:, :], c.ident[:, :], -1.0, None, ALU.mult))
            ch.step(v.tensor_scalar(p.tile_cut[:, :], p.tile_f[:, :], float(NT - 1), None, ALU.min))
            ch.inc(v.memset(p.tile_prev[:, 0:1], 0.0))
            ch.step(v.tensor_copy(p.tile_prev[:, 1:NIP], p.tile_cut[:, 0:NIP - 1]))
            ch.step(v.tensor_tensor(p.begins[:, :], p.tile_cut[:, :], p.tile_prev[:, :], ALU.not_equal))
            ch.step(v.tensor_scalar(p.words_f[:, :], p.tile_prev[:, 0:NIP:GRP], float(1 << GRP), None, ALU.mult))
            for j in range(GRP):
                ch.step(v.scalar_tensor_tensor(p.words_f[:, :], p.begins[:, j:NIP:GRP], float(1 << j),
                                               p.words_f[:, :], ALU.mult, ALU.add))
            ch.inc(v.tensor_copy(c.words[0:1, :], p.words_f[0:1, :]))
            ch.step(v.tensor_tensor(p.upto[0:1, :, :], p.tile_cut[0:1, 0:NI].unsqueeze(1).broadcast_to([1, NT, NI]),
                                    c.lane[0:1, 0:NT].unsqueeze(2).broadcast_to([1, NT, NI]), ALU.is_le))
            ch.step(v.tensor_reduce(p.ends_f[0:1, :], p.upto[0:1, :, :], AX.X, ALU.add))
            ch.step(v.tensor_copy(c.ends[0:1, :], p.ends_f[0:1, :]))

        @block.sync
        def _(sp):
            sp.wait_ge(c.s_dve.sem, c.s_dve.n)
            for k, plane in enumerate((c.col_dst, p.src_plain, c.col_et)):
                sp.dma_start(c.planes[k, :, :], plane[:, :]).then_inc(c.s_store.sem, 16)
            for k, plane in enumerate((c.col_src, c.col_src8)):
                sp.dma_start(c.planes[3 + k, :, :].bitcast(I32), plane[:, :]).then_inc(c.s_store.sem, 16)
            sp.wait_ge(c.s_store.sem, c.s_store.n + 16 * 5)
    c.s_store.n += 16 * 5


def phase_rsqrt(nc, c, out, inp, n):
    dve0, act0 = c.s_dve.n, c.s_scaled.n
    root, sq = c.root[:, 0:n], c.root[:, n:2 * n]
    with nc.Block() as block:

        @block.scalar
        def _(act):
            nc.scalar.activation(root, inp[:, :], ACT.Sqrt).then_inc(c.s_scaled.sem, 1)

        @block.vector
        def _(dve):
            ch = Chain(dve, c.s_dve)
            v = nc.vector
            dve.wait_ge(c.s_scaled.sem, act0 + 1)
            ch.step(v.reciprocal(out[:, :], root))
            for _ in range(2):
                ch.step(v.tensor_tensor(sq, out[:, :], out[:, :], ALU.mult))
                ch.step(v.tensor_tensor(sq, sq, inp[:, :], ALU.mult))
                ch.step(v.tensor_scalar(sq, sq, -0.5, 1.5, ALU.mult, ALU.add))
                ch.step(v.tensor_tensor(out[:, :], out[:, :], sq, ALU.mult))
    c.s_scaled.n += 1


def prepare(nc, c):
    with ExitStack() as ctx:
        p = Core()

        def sb(name, shape, dt=F32):
            return ctx.enter_context(nc.sbuf_tensor(name, shape, dt))

        rows = c.gat[:, :, :].rearrange("p s d -> p (s d)")
        p.src, p.dst, p.et8, p.et200, p.hi_i, p.place_i = (
            rows[:, k * NC:(k + 1) * NC].bitcast(I32) for k in range(6))
        p.edge_no, p.place, p.off = (rows[:, k * NC:(k + 1) * NC] for k in range(6, 9))
        p.hi = rows[:, 9 * NC:10 * NC].bitcast(BF16)[:, 0:NC]
        p.lane_b = sb("p_lane_b", [P, P], BF16)
        p.lo = p.hi
        p.part_no = sb("p_part_no", [P, 1])
        p.zero = sb("p_zero", [P, 1])
        p.lower = sb("p_lower", [P, P])
        p.inb = c.h[:, :, :].rearrange("p t d -> p (t d)")[:, 0:(NT + 1) * NC // 2].bitcast(BF16).rearrange(
            "p (t j) -> p t j", j=NC)
        p.run = c.acc[:, :, :].rearrange("p t d -> p (t d)")[:, 0:(NT + 1) * NC].rearrange(
            "p (t j) -> p t j", j=NC)
        p.before = sb("p_before", [P, NT + 2])
        p.cnt = sb("p_cnt", [P, NT + 1])
        p.base = sb("p_base", [P, NT + 2])
        p.corr = sb("p_corr", [P, NT + 1])
        p.rec_sb = c.xt2[:, :, :].rearrange("p s d -> p (s d)")[:, 0:4 * NC].bitcast(I32).rearrange("p (j k) -> p j k", k=4)
        p.moved = sb("p_moved", [P, 1])
        p.flag = sb("p_flag", [P, 1], I32)
        p.one_place = sb("p_one_place", [P, 1], I32)
        p.spare = sb("p_spare", [P, 1], I32)
        p.one_rec = sb("p_one_rec", [P, 4], I32)
        c.s_copied = Count(ctx, nc, "records_copied")
        c.s_rec = Count(ctx, nc, "record_staged")
        c.s_scat = Count(ctx, nc, "record_scattered")
        phase_constants_and_planes(nc, c, p)

        p.last_dst = sb("p_last_dst", [P, 4], I32)
        p.last_hi = sb("p_last_hi", [P, 4], I32)
        p.visit_no = sb("p_visit_no", [P, NIP])
        p.chunk_no = sb("p_chunk_no", [P, 4])
        p.past = sb("p_past", [P, 4])
        p.leave = sb("p_leave", [P, 4])
        hf = c.acc[:, :, :].rearrange("p t d -> p (t d)")
        p.lo_hot = hf[:, 0:2 * 17 * P // 2].bitcast(BF16).rearrange("p (s k n) -> p s k n", s=2, k=17)
        p.gone = hf[:, 0:4 * NIP].rearrange("p (q n) -> p q n", q=4)
        p.fetched = hf[:, 2048:4096].bitcast(I32).rearrange("p (q n) -> p q n", q=4)
        p.fetched_f = hf[:, 4096:6144].rearrange("p (q k e) -> p q k e", q=4, k=4)
        p.over = sb("p_over", [P, NT])
        p.many = sb("p_many", [P, 1])
        p.deg_loop = sb("p_deg_loop", [P, NT])
        p.chunk_row = c.xs[:, 0:2, :].rearrange("p s d -> p (s d)")
        p.tile_f = c.xs[:, 2:4, :].rearrange("p s d -> p (s d)")
        p.chunk_of = sb("p_chunk_of", [P, 4], I32)
        p.src_f = hf[:, 0:NIP]
        p.dst_f = hf[:, NIP:2 * NIP]
        p.first_f = hf[:, 2 * NIP:3 * NIP]
        p.src_plain = hf[:, 3 * NIP:4 * NIP]
        p.tile_cut = hf[:, 4 * NIP:5 * NIP]
        p.begins = hf[:, 5 * NIP:6 * NIP]
        p.tile_prev = hf[:, 6 * NIP:7 * NIP]
        p.words_f = sb("p_words_f", [P, NIP // GRP])
        p.upto = hf[:, 7 * NIP:7 * NIP + NT * NI // 2].bitcast(F16).rearrange("p (t i) -> p t i", i=NI)
        p.ends_f = sb("p_ends_f", [1, NT])
        c.s_fetch = Count(ctx, nc, "chunks_fetched")
        phase_visits(nc, c, p)
        phase_rsqrt(nc, c, c.dinv, p.deg_loop, NT)


def within_tiles(tile):
    return tile.with_bounds(min_val=0, max_val=NT - 1)


def gather_groups(nc, c, pool, table, index, width):
    st0, mm0 = c.s_stage.n, c.s_mm.n

    def group(g, slot, first):
        if not first:
            pool.wait_ge(c.s_mm.sem, g * GRP + (mm0 + GRP - DEEP * GRP))
        nc.gpsimd.tensor_copy(c.stage[:, slot * GRP:(slot + 1) * GRP],
                              index[:, bass.ds(g * GRP, GRP)]).then_inc(c.s_stage.sem, 1)
        pool.wait_ge(c.s_stage.sem, g + (st0 + 1))
        nc.gpsimd.tensor_tensor(c.idle[:, 0:1], c.node_no[:, 0:1], c.node_no[:, 0:1], ALU.add)
        for j in range(slot * GRP, (slot + 1) * GRP):
            nc.gpsimd.indirect_dma_start(c.gat[:, j, 0:width], None, table,
                                         bass.IndirectOffsetOnAxis(c.stage[:, j:j + 1], 0)
                                         ).then_inc(c.s_gat[j].sem, 16)
    for g in range(DEEP):
        group(g, g, True)
    with pool.Fori(1, NG // DEEP) as it:
        for slot in range(DEEP):
            group(it * DEEP + slot, slot, False)


def phase_edges(nc, c, m, table, index):
    by0 = c.s_by.n
    sel0, mm0, tak0 = c.s_sel.n, c.s_mm.n, c.s_taken.n
    gat0 = [s.n for s in c.s_gat]
    with nc.Block() as block:

        @block.gpsimd
        def _(pool):
            gather_groups(nc, c, pool, table, index, D)

        @block.vector
        def _(dve):
            def group(g, half, first):
                if not first:
                    dve.wait_ge(c.s_mm.sem, g * GRP + (mm0 - GRP))
                nc.vector.tensor_tensor(c.sel[:, half * GRP:(half + 1) * GRP, :],
                                        c.lane[:, :].unsqueeze(1).broadcast_to([P, GRP, P]),
                                        c.col_dst[:, bass.ds(g * GRP, GRP)].unsqueeze(2).broadcast_to([P, GRP, P]),
                                        ALU.is_equal).then_inc(c.s_sel.sem, 1)
                if not (first and half == 0):
                    dve.wait_ge(c.s_by.sem, g * GRP + by0)
                for j in range(GRP):
                    nc.vector.scalar_tensor_tensor(m.junk[:, j, :], c.lane_r[:, :],
                                                   c.col_et[:, bass.ds(g * GRP + j, 1)], m.rel_score[:, :],
                                                   ALU.is_equal, ALU.mult,
                                                   accum_out=m.by_rel[:, bass.ds(g * GRP + j, 1)]
                                                   ).then_inc(c.s_by.sem, 1)
            for half in range(2):
                group(half, half, True)
            with dve.Fori(1, NG // 2) as it:
                for half in range(2):
                    group(it * 2 + half, half, False)

        @block.tensor
        def _(pe):
            def product(j, slot, start):
                nc.tensor.matmul(c.psum[0][:, 0:D], c.sel[:, (slot % 2) * GRP + j, :], c.gat[:, slot * GRP + j, 0:D],
                                 start=start, stop=False, skip_group_check=True).then_inc(c.s_mm.sem, 1)

            def group(g, slot, turn, first):
                word = pe.value_load(c.words[0:1, bass.ds(g, 1)], min_val=0, max_val=NT << GRP)
                tile = word >> GRP
                pe.wait_ge(c.s_sel.sem, g + (sel0 + 1))
                for j in range(GRP):
                    k = slot * GRP + j
                    pe.wait_ge(c.s_gat[k].sem, turn * 16 + (gat0[k] + 16))
                    if first and j == 0:
                        product(j, slot, True)
                        continue
                    begins = (word >> j) & 1
                    with pe.If(begins == 1):
                        pe.wait_ge(c.s_taken.sem, tile + (tak0 + 1))
                        product(j, slot, True)
                    with pe.Else():
                        product(j, slot, False)
                    tile = tile + begins
            for g in range(DEEP):
                group(g, g, 0, g == 0)
            with pe.Fori(1, NG // DEEP) as it:
                for slot in range(DEEP):
                    group(it * DEEP + slot, slot, it, False)

        @block.scalar
        def _(act):
            for t in range(NT):
                end = act.value_load(c.ends[0:1, t:t + 1], min_val=1, max_val=NI)
                act.wait_ge(c.s_mm.sem, end + mm0)
                nc.scalar.copy(c.acc[:, t, 0:D], c.psum[0][:, 0:D]).then_inc(c.s_taken.sem, 1)
    c.s_by.n += NI
    c.s_stage.n += NG
    c.s_sel.n += NG
    c.s_mm.n += NI
    c.s_taken.n += NT
    for s in c.s_gat:
        s.n += 16 * NG // DEEP


def phase_load(nc, c, loads):
    with nc.Block() as block:

        @block.sync
        def _(sp):
            for dst, src in loads:
                sp.dma_start(dst, src).then_inc(c.s_load.sem, 16)
            sp.wait_ge(c.s_load.sem, c.s_load.n + 16 * len(loads))
    c.s_load.n += 16 * len(loads)


def halves(w):
    return w.rearrange("(k p) n -> p k n", p=P)


def each_tile(eng, body):
    with eng.Fori(0, NT // UN) as it:
        for s in range(UN):
            body(it * UN + s, s)


def tile_of(ap, t):
    return ap[:, bass.ds(t, 1), :].rearrange("p o d -> p (o d)")


def col_of(ap, t):
    return ap[:, bass.ds(t, 1)]


def sweeps(dve, c, ch):
    def sweep(step):
        with dve.Fori(0, NT // UN) as it:
            for s in range(UN):
                step(it * UN + s, s).then_inc(c.s_dve.sem, 1)
        c.s_dve.n += NT
        ch.wait()
    return sweep


def phase_norm(nc, c, from_dram=None, loads=(), to_dram=None, magnitudes=False):
    groups = [slice(g * UN, (g + 1) * UN) for g in range(NT // UN)]
    row0 = [x.n for x in c.s_back]
    with nc.Block() as block:

        @block.sync
        def _(sp):
            if from_dram is not None:
                for g, tiles in enumerate(groups):
                    for buf, source in ((c.x, from_dram[0]), (c.h, from_dram[1])):
                        sp.dma_start(buf[:, tiles, :], tiles_view(source)[:, tiles, :]).then_inc(c.s_back[g].sem, 16)
            for dst, src in loads:
                sp.dma_start(dst, src).then_inc(c.s_load.sem, 16)
            if loads:
                sp.wait_ge(c.s_load.sem, c.s_load.n + 16 * len(loads))

        @block.vector
        def _(dve):
            v = nc.vector
            ch = Chain(dve, c.s_dve)
            for g, tiles in enumerate(groups):
                if from_dram is not None:
                    dve.wait_ge(c.s_back[g].sem, row0[g] + 32)
                ch.step(v.tensor_tensor(c.x[:, tiles, :], c.x[:, tiles, :], c.h[:, tiles, :], ALU.add))
                for t in range(g * UN, (g + 1) * UN):
                    ch.inc(v.bn_stats(c.stats[:, t, :], c.x[:, t, :]))
                ch.wait()
                for t in range(g * UN, (g + 1) * UN):
                    ch.inc(v.bn_aggr(c.mv[:, t, :], c.stats[:, t, :]))
            ch.wait()
            ch.step(v.tensor_scalar(c.var[:, :], c.mv[:, :, 1], EPS, None, ALU.add))
    if from_dram is not None:
        for x in c.s_back:
            x.n += 32
    c.s_load.n += 16 * len(loads)
    phase_rsqrt(nc, c, c.rstd, c.var, NT)
    dve0 = c.s_dve.n
    step = UN + (1 if magnitudes else 0)
    parts = len(groups) + 1 if to_dram is not None and to_dram.shape[0] == N else len(groups)
    with nc.Block() as block:

        @block.vector
        def _(dve):
            v = nc.vector
            ch = Chain(dve, c.s_dve)
            for g, tiles in enumerate(groups):
                for t in range(g * UN, (g + 1) * UN):
                    ch.inc(v.tensor_scalar(c.x[:, t, :], c.x[:, t, :], c.mv[:, t, 0:1], c.rstd[:, t:t + 1],
                                           ALU.subtract, ALU.mult))
                if magnitudes:
                    ch.wait()
                    ch.inc(v.tensor_reduce(c.amax[:, tiles], c.x[:, tiles, :], AX.X, ALU.max,
                                           apply_absolute_value=True))

        @block.sync
        def _(sp):
            if to_dram is not None:
                whole = to_dram.shape[0] // P
                for g in range(len(groups)):
                    sp.wait_ge(c.s_dve.sem, dve0 + step * (g + 1))
                    tiles = slice(g * UN, min((g + 1) * UN, whole))
                    sp.dma_start(to_dram[tiles.start * P:tiles.stop * P, :].rearrange("(t p) d -> p t d", p=P),
                                 c.x[:, tiles, :]).then_inc(c.s_store.sem, 16)
                if whole < NT:
                    sp.dma_start(to_dram[whole * P:N, :], c.x[0:LAST, whole, :]).then_inc(c.s_store.sem, 16)
                sp.wait_ge(c.s_store.sem, c.s_store.n + 16 * parts)
    if to_dram is not None:
        c.s_store.n += 16 * parts


def phase_start(nc, c):
    with nc.Block() as block:

        @block.vector
        def _(dve):
            ch = Chain(dve, c.s_dve)
            ch.step(nc.vector.memset(c.x[:, NT - 1, :], 0.0))
            nc.vector.memset(c.valid[:, :], 0.0).then_inc(c.s_add.sem, 1)

        @block.gpsimd
        def _(pool):
            ch = Chain(pool, c.s_pool)
            ch.inc(nc.gpsimd.iota(c.node_no[:, :], [[0, P]], base=0, channel_multiplier=1,
                                  allow_small_or_imprecise_dtypes=True))
            ch.step(nc.gpsimd.iota(c.lane_r[:, :], [[1, R]], base=0, channel_multiplier=0,
                                   allow_small_or_imprecise_dtypes=True))
    c.s_add.n += 1


def phase_relation_table(nc, c):
    QB = NREL * D // 512
    sc0, tr0, xt0, lin0, out0, st0 = (s.n for s in (c.s_scaled, c.s_tr, c.s_xt, c.s_lin, c.s_out, c.s_store))
    slot0 = [s.n for s in c.s_slot]
    banks_t = [c.psum[s // 2][:, (s % 2) * D:(s % 2 + 1) * D] for s in range(UN)]
    rows = c.acc[:, :, :].rearrange("p t d -> p (t d)")[:, 0:UN * NREL * D].rearrange("p (s n) -> p s n", s=UN)
    dram = c.rtab.rearrange("(n r) d -> n (r d)", r=NREL)
    with nc.Block() as block:

        @block.scalar
        def _(act):
            def body(t, s, early):
                if not early:
                    act.wait_ge(c.s_tr.sem, t + (tr0 + 1 - UN))
                nc.scalar.copy(c.xs[:, s, :], tile_of(c.x, t)).then_inc(c.s_scaled.sem, 1)
                act.wait_ge(c.s_tr.sem, t + (tr0 + 1))
                if not early:
                    act.wait_ge(c.s_lin.sem, t * QB + (lin0 + QB * (1 - UN)))
                nc.scalar.copy(c.xt[:, s, :], banks_t[s]).then_inc(c.s_xt.sem, 1)
                if not early:
                    act.wait_ge(c.s_slot[s].sem, turn_of(t) * 16 + slot0[s])
                for q in range(0, QB, 2):
                    act.wait_ge(c.s_lin.sem, t * QB + (lin0 + q + 1))
                    nc.scalar.copy(rows[:, s, q * 512:(q + 1) * 512], c.psum[3 + q][:, :]).then_inc(c.s_out.sem, 1)

            unrolled(act, body)

        @block.vector
        def _(dve):
            def body(t, s, early):
                if not early:
                    dve.wait_ge(c.s_slot[s].sem, turn_of(t) * 16 + slot0[s])
                for q in range(1, QB, 2):
                    dve.wait_ge(c.s_lin.sem, t * QB + (lin0 + q + 1))
                    nc.vector.tensor_copy(rows[:, s, q * 512:(q + 1) * 512], c.psum[3 + q][:, :]
                                          ).then_inc(c.s_odd.sem, 1)

            unrolled(dve, body)

        @block.tensor
        def _(pe):
            def body(t, s, early):
                pe.wait_ge(c.s_scaled.sem, t + (sc0 + 1))
                if not early:
                    pe.wait_ge(c.s_xt.sem, t + (xt0 + 1 - UN))
                for k in range(2):
                    ins = nc.tensor.transpose(banks_t[s][:, k * P:(k + 1) * P], c.xs[:, s, k * P:(k + 1) * P],
                                              c.ident[:, :])
                ins.then_inc(c.s_tr.sem, 1)
                pe.wait_ge(c.s_xt.sem, t + (xt0 + 1))
                for q in range(QB):
                    if not (early and s == 0):
                        done = (c.s_out, out0) if q % 2 == 0 else (c.s_odd, c.s_odd.n)
                        pe.wait_ge(done[0].sem, t * (QB // 2) + (done[1] + q // 2 + 1 - QB // 2))
                    for k in range(2):
                        ins = nc.tensor.matmul(c.psum[3 + q][:, :], c.xt[:, s, k * P:(k + 1) * P],
                                               c.w[:, k, q * 512:(q + 1) * 512], start=k == 0, stop=k == 1)
                    ins.then_inc(c.s_lin.sem, 1)

            unrolled(pe, body)

        @block.sync
        def _(sp):
            def body(t, s, early):
                sp.wait_ge(c.s_out.sem, t * (QB // 2) + (out0 + QB // 2))
                sp.wait_ge(c.s_odd.sem, t * (QB // 2) + (c.s_odd.n + QB // 2))
                sp.dma_start(dram[t * P:(t + 1) * P, :], rows[:, s, :]).then_inc(c.s_slot[s].sem, 16)

            for t in range(NT):
                body(t, t % UN, False)
            for s in range(UN):
                sp.wait_ge(c.s_slot[s].sem, slot0[s] + 16 * (NT // UN))
    for s in (c.s_scaled, c.s_tr, c.s_xt):
        s.n += NT
    c.s_lin.n += NT * QB
    c.s_out.n += NT * QB // 2
    c.s_odd.n += NT * QB // 2
    for s in c.s_slot:
        s.n += 16 * (NT // UN)


class Turn:
    now = 0


def turn_of(t):
    return Turn.now


def unrolled(eng, body):
    Turn.now = 0
    for s in range(UN):
        body(s, s, True)
    with eng.Fori(1, NT // UN) as it:
        Turn.now = it
        for s in range(UN):
            body(it * UN + s, s, False)


def phase_batch_norm(nc, c):
    pe0, dve0 = c.s_pe.n, c.s_dve.n

    def sums(data, tail):
        with nc.Block() as block:

            @block.tensor
            def _(pe):
                nc.tensor.matmul(c.psum[0][:, 0:D], c.ones[:, :], data[:, 0, :], start=True, stop=False)
                for t in range(1, NT):
                    ins = nc.tensor.matmul(c.psum[0][:, 0:D], tail if t == NT - 1 else c.ones[:, :],
                                           data[:, t, :], start=False, stop=t == NT - 1)
                ins.then_inc(c.s_pe.sem, 1)
        c.s_pe.n += 1

    sums(c.accd, c.ones[:, :])
    with nc.Block() as block:

        @block.vector
        def _(dve):
            v = nc.vector
            ch = Chain(dve, c.s_dve)
            sweep = sweeps(dve, c, ch)
            ch.inc(v.tensor_scalar(c.valid[:, :], c.node_no[:, :], float(LAST), None, ALU.is_lt))
            ch.step(v.tensor_scalar(c.mean[:, :], c.psum[0][:, 0:D], 1.0 / N, None, ALU.mult))
            sweep(lambda t, s: v.tensor_tensor(tile_of(c.accd, t), tile_of(c.accd, t), c.mean[:, :], ALU.subtract))
            sweep(lambda t, s: v.tensor_tensor(tile_of(c.h, t), tile_of(c.accd, t), tile_of(c.accd, t), ALU.mult))
    sums(c.h, c.valid[:, :])
    with nc.Block() as block:

        @block.vector
        def _(dve):
            ch = Chain(dve, c.s_dve)
            ch.step(nc.vector.tensor_scalar(c.mean[:, :], c.psum[0][:, 0:D], 1.0 / N, EPS, ALU.mult, ALU.add))
    phase_rsqrt(nc, c, c.gain, c.mean, D)
    with nc.Block() as block:

        @block.vector
        def _(dve):
            v = nc.vector
            ch = Chain(dve, c.s_dve)
            sweep = sweeps(dve, c, ch)
            ch.step(v.tensor_tensor(c.gain[:, :], c.gain[:, :], c.bias[:, 0, :], ALU.mult))
            sweep(lambda t, s: v.tensor_tensor(tile_of(c.h, t), tile_of(c.accd, t), c.gain[:, :], ALU.mult))
            sweep(lambda t, s: v.tensor_tensor(tile_of(c.h, t), tile_of(c.h, t), c.bias[:, 1, :], ALU.add))


def phase_to_table(nc, c, source, table, width):
    st0 = c.s_store.n
    with nc.Block() as block:

        @block.sync
        def _(sp):
            sp.dma_start(table.rearrange("(t p) d -> p t d", p=P), source).then_inc(c.s_store.sem, 16)
            sp.wait_ge(c.s_store.sem, st0 + 16)

        @block.vector
        def _(dve):
            ch = Chain(dve, c.s_dve)
            if width > D:
                dve.wait_ge(c.s_store.sem, st0 + 16)
            ch.step(nc.vector.memset(c.acc[:, :, 0:width], 0.0))
    c.s_store.n += 16


def transpose_relations(nc, c, m):
    rest = R - P
    for k in range(2):
        nc.tensor.transpose(c.psum[0][:, k * D:k * D + P], m.rel[:, 0, k * P:(k + 1) * P], c.ident[:, :])
        ins = nc.tensor.transpose(c.psum[0][:, k * D + P:k * D + R], m.rel[0:rest, 1, k * P:(k + 1) * P],
                                  c.ident[0:rest, 0:rest])
    return ins


def relation_loads(c, m):
    return [(m.rel[:, 0, :], c.ins["L3_gnn_rel_emb"][0:P, :]), (m.rel[0:R - P, 1, :], c.ins["L3_gnn_rel_emb"][P:R, :])]


def phase_relation_scores(nc, c, m):
    pe0, act0 = c.s_pe.n, c.s_scaled.n
    w3 = c.acc[:, :, :].rearrange("p t d -> p (t d)")[:, 0:6 * 3 * D].rearrange("p (q n) -> p q n", q=6)
    a_row = c.h[:, 0:3, :].rearrange("p t d -> p (t d)")
    phase_load(nc, c, [(w3, c.ins["L3_gnn_W3"].rearrange("(q p) n -> p q n", p=P)),
                       (a_row, c.ins["L3_gnn_a"].rearrange("n o -> o n").to_broadcast([P, 3 * D]))] +
               relation_loads(c, m))
    with nc.Block() as block:

        @block.vector
        def _(dve):
            v = nc.vector
            ch = Chain(dve, c.s_dve)
            for q in range(6):
                ch.step(v.tensor_tensor_reduce(out=c.h[:, 4:7, :].rearrange("p t d -> p (t d)"), in0=w3[:, q, :],
                                               in1=a_row, scale=1.0, scalar=0.0, op0=ALU.mult, op1=ALU.add,
                                               accum_out=c.wv[:, q:q + 1]))
            for q in range(2):
                ch.inc(v.tensor_copy(m.wide[:, q, :], c.wv[:, 4 + q:5 + q].to_broadcast([P, P])))

        @block.tensor
        def _(pe):
            transpose_relations(nc, c, m).then_inc(c.s_pe.sem, 1)

        @block.scalar
        def _(act):
            act.wait_ge(c.s_pe.sem, pe0 + 1)
            for k in range(2):
                ins = nc.scalar.copy(m.rel_t[:, k, :], c.psum[0][:, k * D:k * D + R])
            ins.then_inc(c.s_scaled.sem, 1)
    c.s_pe.n += 1
    c.s_scaled.n += 1
    with nc.Block() as block:

        @block.tensor
        def _(pe):
            for k in range(2):
                ins = nc.tensor.matmul(c.psum[1][:, 0:R], m.wide[:, k, :], m.rel_t[:, k, :], start=k == 0, stop=k == 1)
            ins.then_inc(c.s_pe.sem, 1)

        @block.vector
        def _(dve):
            ch = Chain(dve, c.s_dve)
            dve.wait_ge(c.s_pe.sem, c.s_pe.n + 1)
            ch.inc(nc.vector.tensor_copy(m.rel_score[:, :], c.psum[1][:, 0:R]))
            ch.inc(nc.vector.memset(m.by_rel[:, NI:NIP], 0.0))
    c.s_pe.n += 1


def phase_attention_weights(nc, c, m):
    pe0, act0 = c.s_pe.n, c.s_scaled.n
    rest = R - P
    phase_load(nc, c, [(c.w[:, :, 0:D], halves(c.ins["L3_gnn_weight_neighbor"])),
                       (c.w[:, :, D:2 * D], halves(c.ins["L3_gnn_loop_weight"])),
                       (c.w[:, :, 2 * D:3 * D], halves(c.ins["L3_gnn_evolve_loop_weight"]))] + relation_loads(c, m))
    with nc.Block() as block:

        @block.vector
        def _(dve):
            v = nc.vector
            ch = Chain(dve, c.s_dve)
            for q in range(2):
                ch.inc(v.tensor_copy(m.wide[:, q, :], c.wv[:, 2 + q:3 + q].to_broadcast([P, P])))
            ch.inc(v.tensor_scalar(c.col_et[:, :], c.col_et[:, :], -1.0, None, ALU.mult))
            ch.inc(v.tensor_copy(c.accd, c.x[:, :, :]))
            ch.inc(v.memset(c.acc[:, :, D:D + 4], 0.0))
            dve.wait_ge(c.s_pe.sem, pe0 + 2)
            ch.inc(v.tensor_copy(m.rel_w[:, 0, :], c.psum[2][:, 0:D]))
            ch.inc(v.tensor_copy(m.rel_w[0:rest, 1, :], c.psum[3][0:rest, 0:D]))

        @block.tensor
        def _(pe):
            transpose_relations(nc, c, m).then_inc(c.s_pe.sem, 1)
            pe.wait_ge(c.s_scaled.sem, act0 + 1)
            for k in range(2):
                nc.tensor.matmul(c.psum[2][:, 0:D], m.rel_t[:, k, 0:P], c.w[:, k, 0:D], start=k == 0, stop=k == 1)
            for k in range(2):
                ins = nc.tensor.matmul(c.psum[3][0:rest, 0:D], m.rel_t[:, k, P:R], c.w[:, k, 0:D],
                                       start=k == 0, stop=k == 1)
            ins.then_inc(c.s_pe.sem, 1)

        @block.scalar
        def _(act):
            act.wait_ge(c.s_pe.sem, pe0 + 1)
            for k in range(2):
                ins = nc.scalar.copy(m.rel_t[:, k, :], c.psum[0][:, k * D:k * D + R])
            ins.then_inc(c.s_scaled.sem, 1)
    c.s_pe.n += 2
    c.s_scaled.n += 1


def phase_node_scores(nc, c, m):
    tr0, xt0, lin0, out0 = (s.n for s in (c.s_tr, c.s_xt, c.s_lin, c.s_out))
    banks = [c.psum[t][:, 0:D] for t in range(4)]
    with nc.Block() as block:

        @block.scalar
        def _(act):
            for t in range(NT):
                act.wait_ge(c.s_tr.sem, tr0 + t + 1)
                if t >= 4:
                    act.wait_ge(c.s_lin.sem, lin0 + t - 3)
                nc.scalar.copy(c.xt[:, t % 4, :], banks[t % 4]).then_inc(c.s_xt.sem, 1)

        @block.tensor
        def _(pe):
            def transposes(t):
                if t >= 4:
                    pe.wait_ge(c.s_xt.sem, xt0 + t - 3)
                for k in range(2):
                    ins = nc.tensor.transpose(banks[t % 4][:, k * P:(k + 1) * P], c.x[:, t, k * P:(k + 1) * P],
                                              c.ident[:, :])
                ins.then_inc(c.s_tr.sem, 1)

            def products(t):
                bank = c.psum[4 + t % 4]
                pe.wait_ge(c.s_xt.sem, xt0 + t + 1)
                if t >= 4:
                    pe.wait_ge(c.s_out.sem, out0 + t - 3)
                for k in range(2):
                    nc.tensor.matmul(bank[:, P:P + 1], c.xt[:, t % 4, k * P:(k + 1) * P], c.wv[:, k:k + 1],
                                     start=k == 0, stop=k == 1)
                for k in range(2):
                    ins = nc.tensor.matmul(bank[:, 0:P], m.wide[:, k, :], c.xt[:, t % 4, k * P:(k + 1) * P],
                                           start=k == 0, stop=k == 1)
                ins.then_inc(c.s_lin.sem, 1)
            transposes(0)
            transposes(1)
            for t in range(NT):
                if t + 2 < NT:
                    transposes(t + 2)
                products(t)

        @block.vector
        def _(dve):
            for t in range(NT):
                bank = c.psum[4 + t % 4]
                dve.wait_ge(c.s_lin.sem, lin0 + t + 1)
                nc.vector.tensor_copy(m.dst_score[:, t * P:(t + 1) * P], bank[:, 0:P])
                nc.vector.tensor_copy(c.acc[:, t, D:D + 1], bank[:, P:P + 1]).then_inc(c.s_out.sem, 1)
    for s in (c.s_tr, c.s_xt, c.s_lin, c.s_out):
        s.n += NT


def phase_attention_edges(nc, c, m):
    sel0, mm0, tak0, al0, sco0, rel0, dve0 = (s.n for s in (c.s_sel, c.s_mm, c.s_taken, c.s_alpha, c.s_score,
                                                           c.s_rel, c.s_dve))
    gat0 = [s.n for s in c.s_gat]
    hot0, by0, cols0 = c.s_hot.n, c.s_by.n, c.s_cols.n
    with nc.Block() as block:

        @block.gpsimd
        def _(pool):
            gather_groups(nc, c, pool, c.ltab, c.col_src, D + 4)

        @block.scalar
        def _(act):
            def relations(g, half, first):
                if not first:
                    act.wait_ge(c.s_mm.sem, g * GRP + (mm0 - GRP))
                for j in range(GRP):
                    nc.scalar.activation(m.rel_hot[:, half * GRP + j, :], m.lane_r[:, :], ACT.Square,
                                         bias=c.col_et[:, bass.ds(g * GRP + j, 1)]).then_inc(c.s_rel.sem, 1)
                act.wait_ge(c.s_rel.sem, g * GRP + (rel0 + GRP))
                hot = m.rel_hot[:, half * GRP:(half + 1) * GRP, :]
                nc.scalar.activation(hot, hot, ACT.Relu, bias=c.ones[:, 0:1], scale=-1.0).then_inc(c.s_hot.sem, 1)

            def exponent(g, half):
                act.wait_ge(c.s_score.sem, g + (sco0 + 1))
                nc.scalar.activation(m.expo[:, half, :], m.score[:, half, :], ACT.Exp).then_inc(c.s_alpha.sem, 1)

            def take(g, first):
                word = act.value_load(c.words[0:1, bass.ds(g, 1)], min_val=0, max_val=NT << GRP)
                with act.If((word & ((1 << GRP) - 1)) != 0):
                    tile = word >> GRP
                    for j in range(1 if first else 0, GRP):
                        begins = (word >> j) & 1
                        with act.If(begins == 1):
                            act.wait_ge(c.s_mm.sem, g * GRP + (mm0 + j))
                            into = c.acc[:, bass.ds(within_tiles(tile), 1), :].rearrange("p o d -> p (o d)")
                            nc.scalar.copy(into, c.psum[0][:, 0:D + R]).then_inc(c.s_taken.sem, 1)
                        tile = tile + begins

            relations(0, 0, True)
            exponent(0, 0)
            relations(1, 1, True)
            exponent(1, 1)
            take(0, True)
            with act.Fori(1, NG // 2) as it:
                for half in range(2):
                    exponent(it * 2 + half, half)
                    take(it * 2 + (half - 1), False)
                    relations(it * 2 + half, half, False)
            take(NG - 1, False)
            act.wait_ge(c.s_mm.sem, mm0 + NI)
            nc.scalar.copy(c.acc[:, NT - 1, :], c.psum[0][:, 0:D + R]).then_inc(c.s_taken.sem, 1)

        @block.vector
        def _(dve):
            v = nc.vector

            def read_off(g, half, first):
                if not first:
                    dve.wait_ge(c.s_sel.sem, g * GRP + (sel0 - GRP))
                v.tensor_copy(m.cols[:, half, :], c.col_dst[:, bass.ds(g * GRP, GRP)]).then_inc(c.s_cols.sem, 1)
                word = dve.value_load(c.words[0:1, bass.ds(g, 1)], min_val=0, max_val=NT << GRP)
                dve.wait_ge(c.s_cols.sem, g + (cols0 + 1))
                tile = word >> GRP
                for j in range(GRP):
                    tile = tile + ((word >> j) & 1)
                    v.scalar_tensor_tensor(m.junk_dst[:, j, :], c.lane[:, :], m.cols[:, half, j:j + 1],
                                           m.dst_score[:, bass.ds(within_tiles(tile) * P, P)], ALU.is_equal, ALU.mult,
                                           accum_out=m.by_dst[:, half, j:j + 1]).then_inc(c.s_by.sem, 1)

            def group(g, slot, turn, first):
                half = slot % 2
                at = g * 5 + dve0

                def chained(k, ins):
                    ins.then_inc(c.s_dve.sem, 1)
                    dve.wait_ge(c.s_dve.sem, at + k)
                dve.wait_ge(c.s_by.sem, g * GRP + (by0 + GRP))
                chained(1, v.tensor_tensor(m.score[:, half, :], m.by_dst[:, half, :],
                                           m.by_rel[:, bass.ds(g * GRP, GRP)], ALU.add))
                for j in range(GRP):
                    k = slot * GRP + j
                    dve.wait_ge(c.s_gat[k].sem, turn * 16 + (gat0[k] + 16))
                chained(2, v.tensor_tensor(m.score[:, half, :], m.score[:, half, :],
                                           c.gat[:, slot * GRP:(slot + 1) * GRP, D], ALU.add))
                chained(3, v.tensor_scalar(m.leak[:, half, :], m.score[:, half, :], 0.01, None, ALU.mult))
                v.tensor_tensor(m.score[:, half, :], m.score[:, half, :], m.leak[:, half, :], ALU.max
                                ).then_inc(c.s_score.sem, 1)
                read_off(g + 1, 1 - half, False)
                dve.wait_ge(c.s_alpha.sem, g + (al0 + 1))
                chained(4, v.reciprocal(m.alpha[:, half, :], m.expo[:, half, :]))
                chained(5, v.tensor_tensor(m.alpha[:, half, :], m.alpha[:, half, :], m.expo[:, half, :], ALU.mult))
                if not first:
                    dve.wait_ge(c.s_mm.sem, g * GRP + (mm0 - GRP))
                for j in range(GRP):
                    v.tensor_scalar(c.sel[:, half * GRP + j, :], c.lane[:, :], m.cols[:, half, j:j + 1],
                                    m.alpha[:, half, j:j + 1], ALU.is_equal, ALU.mult).then_inc(c.s_sel.sem, 1)

            read_off(0, 0, True)
            for g in range(DEEP):
                group(g, g, 0, g < 2)
            with dve.Fori(1, NG // DEEP) as it:
                for slot in range(DEEP):
                    group(it * DEEP + slot, slot, it, False)

        @block.tensor
        def _(pe):
            def products(j, slot, start):
                sel, k = c.sel[:, (slot % 2) * GRP + j, :], slot * GRP + j
                nc.tensor.matmul(c.psum[0][:, 0:D], sel, c.gat[:, k, 0:D], start=start, stop=False,
                                 skip_group_check=True)
                nc.tensor.matmul(c.psum[0][:, D:D + R], sel, m.rel_hot[:, (slot % 2) * GRP + j, :], start=False,
                                 stop=False, skip_group_check=True).then_inc(c.s_mm.sem, 1)

            def group(g, slot, turn, first):
                word = pe.value_load(c.words[0:1, bass.ds(g, 1)], min_val=0, max_val=NT << GRP)
                tile = word >> GRP
                pe.wait_ge(c.s_hot.sem, g + (hot0 + 1))
                for j in range(GRP):
                    k = slot * GRP + j
                    pe.wait_ge(c.s_gat[k].sem, turn * 16 + (gat0[k] + 16))
                    pe.wait_ge(c.s_sel.sem, g * GRP + (sel0 + j + 1))
                    if first and j == 0:
                        products(j, slot, True)
                        continue
                    begins = (word >> j) & 1
                    with pe.If(begins == 1):
                        pe.wait_ge(c.s_taken.sem, tile + (tak0 + 1))
                        products(j, slot, True)
                    with pe.Else():
                        products(j, slot, False)
                    tile = tile + begins
            for g in range(DEEP):
                group(g, g, 0, g == 0)
            with pe.Fori(1, NG // DEEP) as it:
                for slot in range(DEEP):
                    group(it * DEEP + slot, slot, it, False)
    c.s_stage.n += NG
    c.s_sel.n += NI
    c.s_mm.n += NI
    c.s_taken.n += NT
    c.s_alpha.n += NG
    c.s_score.n += NG
    c.s_rel.n += NI
    c.s_hot.n += NG
    c.s_cols.n += NG + 1
    c.s_by.n += (NG + 1) * GRP
    c.s_dve.n += NG * 5
    for s in c.s_gat:
        s.n += 16 * NG // DEEP


def phase_attention_linear(nc, c, m):
    sc0, tr0, xt0, lin0, out0, dve0 = (s.n for s in (c.s_scaled, c.s_tr, c.s_xt, c.s_lin, c.s_out, c.s_dve))
    rest = R - P
    banks = [(c.psum[0], c.psum[1], c.psum[2], c.psum[3]), (c.psum[4], c.psum[5], c.psum[6], c.psum[7])]
    with nc.Block() as block:

        @block.vector
        def _(dve):
            ch = Chain(dve, c.s_dve)
            v = nc.vector
            ch.step(v.tensor_scalar(m.no_in[:, :], c.has_in[:, :], -1.0, 1.0, ALU.mult, ALU.add))
            first = c.s_dve.n
            for t in range(NT):
                b = banks[t % 2]
                if t >= 2:
                    dve.wait_ge(c.s_tr.sem, tr0 + t - 1)
                dve.wait_ge(c.s_lin.sem, lin0 + t + 1)
                v.tensor_scalar(c.tmp[:, t % 2, :], b[2][:, 0:D], 0.0, None, ALU.max).then_inc(c.s_dve.sem, 1)
                dve.wait_ge(c.s_dve.sem, first + 2 * t + 1)
                v.scalar_tensor_tensor(c.h[:, t, :], b[3][:, 0:D], c.has_in[:, t:t + 1], c.tmp[:, t % 2, :],
                                       ALU.mult, ALU.add).then_inc(c.s_dve.sem, 1)
                dve.wait_ge(c.s_dve.sem, first + 2 * t + 2)
                v.scalar_tensor_tensor(c.h[:, t, :], b[3][:, D:2 * D], m.no_in[:, t:t + 1], c.h[:, t, :],
                                       ALU.mult, ALU.add).then_inc(c.s_out.sem, 1)
            c.s_dve.n += 2 * NT

        @block.scalar
        def _(act):
            for t in range(NT):
                b = banks[t % 2]
                if t >= 2:
                    act.wait_ge(c.s_lin.sem, lin0 + t - 1)
                act.wait_ge(c.s_tr.sem, tr0 + t + 1)
                nc.scalar.copy(m.xt3[:, t % 2, 0:2 * D], b[0][:, :])
                nc.scalar.copy(m.xt3[:, t % 2, 2 * D:3 * D], b[1][:, 0:D]).then_inc(c.s_xt.sem, 1)

        @block.tensor
        def _(pe):
            def transposes(t):
                b = banks[t % 2]
                if t >= 2:
                    pe.wait_ge(c.s_xt.sem, xt0 + t - 1)
                for k in range(2):
                    nc.tensor.transpose(b[0][:, k * P:(k + 1) * P], c.acc[:, t, k * P:(k + 1) * P], c.ident[:, :])
                nc.tensor.transpose(b[0][:, D:D + P], c.acc[:, t, D:D + P], c.ident[:, :])
                nc.tensor.transpose(b[0][0:rest, D + P:2 * D], c.acc[:, t, D + P:D + R], c.ident[:, :])
                for k in range(2):
                    ins = nc.tensor.transpose(b[1][:, k * P:(k + 1) * P], c.x[:, t, k * P:(k + 1) * P], c.ident[:, :])
                ins.then_inc(c.s_tr.sem, 1)

            def products(t):
                b = banks[t % 2]
                pe.wait_ge(c.s_xt.sem, xt0 + t + 1)
                if t >= 2:
                    pe.wait_ge(c.s_out.sem, out0 + t - 1)
                xt = m.xt3[:, t % 2, :]
                for k in range(2):
                    nc.tensor.matmul(b[2][:, 0:D], xt[:, k * P:(k + 1) * P], c.w[:, k, 0:D], start=k == 0, stop=False)
                nc.tensor.matmul(b[2][:, 0:D], xt[:, D:D + P], m.rel_w[:, 0, :], start=False, stop=False)
                nc.tensor.matmul(b[2][:, 0:D], xt[0:rest, D + P:2 * D], m.rel_w[0:rest, 1, :], start=False, stop=True)
                for k in range(2):
                    ins = nc.tensor.matmul(b[3][:, :], xt[:, 2 * D + k * P:2 * D + (k + 1) * P], c.w[:, k, D:3 * D],
                                           start=k == 0, stop=k == 1)
                ins.then_inc(c.s_lin.sem, 1)
            transposes(0)
            for t in range(NT):
                if t + 1 < NT:
                    transposes(t + 1)
                products(t)
    for s in (c.s_tr, c.s_xt, c.s_lin, c.s_out):
        s.n += NT


def dense_memory(nc, ctx, c, part):
    def sb(name, shape, dt=F32):
        return ctx.enter_context(nc.sbuf_tensor(f"{name}_{part}", shape, dt))

    c.at = sb("counts_t", [P, NT, NT * P], F16)
    c.hs = sb("h_split", [P, NT, 2 * D], F16)
    c.raw = sb("work", [P, 4352])
    c.rest = sb("count_rest", [P, NT * P], F16)
    c.biggest = sb("biggest", [P, 4])
    c.scale_i = sb("scale_bits", [P, 3], I32)
    c.factor = sb("factor", [P, NT])


def phase_build_counts(nc, c):
    GS = GRP
    flat = c.raw
    lane16 = flat[:, 0:NT * P // 2].bitcast(I16)
    o = NT * P // 2
    col_dst, col_src = flat[:, o:o + NIP], flat[:, o + NIP:o + 2 * NIP]
    dst_hot = flat[:, o + 2 * NIP:o + 2 * NIP + 2 * GS * P // 2].bitcast(F16).rearrange(
        "p (s j n) -> p s j n", s=2, j=GS)
    RING = 4
    src_hot = c.hs[:, :, :].rearrange("p t d -> p (t d)").rearrange("p (s n) -> p s n", s=RING)
    per_bank = 512 // P
    NB = -(-NT // per_bank)
    load0, pool0, sel0, hot0, vis0, tak0 = (x.n for x in (c.s_load, c.s_pool, c.s_sel, c.s_hot, c.s_visit, c.s_taken))
    with nc.Block() as block:

        @block.sync
        def _(sp):
            for dst, k in ((col_dst, 0), (col_src, 1)):
                sp.dma_start(dst, c.planes[k, :, :]).then_inc(c.s_load.sem, 16)
            for k, (dst, src) in enumerate(counts_parts(c)):
                sp.wait_ge(c.s_taken.sem, tak0 + NB * UN * (k + 1))
                sp.dma_start(dst, src).then_inc(c.s_keep.sem, 16)

        @block.gpsimd
        def _(pool):
            nc.gpsimd.iota(lane16, [[1, NT * P]], base=0, channel_multiplier=0,
                           allow_small_or_imprecise_dtypes=True).then_inc(c.s_pool.sem, 1)

        @block.vector
        def _(dve):
            dve.wait_ge(c.s_load.sem, load0 + 32)
            dve.wait_ge(c.s_pool.sem, pool0 + 1)

            def group(g, half, first):
                if not (first and half < 2):
                    dve.wait_ge(c.s_visit.sem, g * GS + (vis0 - GS))
                nc.vector.tensor_tensor(dst_hot[:, half, :, :],
                                        c.lane[:, :].unsqueeze(1).broadcast_to([P, GS, P]),
                                        col_dst[:, bass.ds(g * GS, GS)].unsqueeze(2).broadcast_to([P, GS, P]),
                                        ALU.is_equal).then_inc(c.s_sel.sem, 1)
                for j in range(GS):
                    if not (first and half == 0 and j < RING):
                        dve.wait_ge(c.s_visit.sem, g * GS + (vis0 + j + 1 - RING))
                    nc.vector.tensor_scalar(src_hot[:, j % RING, :], lane16, col_src[:, bass.ds(g * GS + j, 1)],
                                            None, ALU.is_equal).then_inc(c.s_hot.sem, 1)
            for half in range(2):
                group(half, half, True)
            with dve.Fori(1, NG // 2) as it:
                for half in range(2):
                    group(it * 2 + half, half, False)

        @block.tensor
        def _(pe):
            heavy = pe.value_load(c.heavy[0:1, 0:1], min_val=0, max_val=1)

            def leave_rest(tile):
                for k in range(NT):
                    b = k // per_bank
                    if k % per_bank == 0:
                        pe.wait_ge(c.s_round.sem, tile * NB + (b + 1))
                    ins = nc.tensor.matmul(c.psum[b][:, (k % per_bank) * P:(k % per_bank + 1) * P], c.minus16[:, :],
                                           c.at[:, k, bass.ds(tile * P, P)], start=False, stop=False,
                                           skip_group_check=True)
                    if k % per_bank == per_bank - 1 or k == NT - 1:
                        ins.then_inc(c.s_less.sem, 1)

            def products(j, half, start, ended):
                for k in range(NT):
                    b = k // per_bank
                    if ended is not None and k % per_bank == 0:
                        pe.wait_ge(c.s_taken.sem, ended * NB + (tak0 + b + 1))
                    ins = nc.tensor.matmul(c.psum[b][:, (k % per_bank) * P:(k % per_bank + 1) * P],
                                           src_hot[:, j % RING, k * P:(k + 1) * P], dst_hot[:, half, j, :],
                                           start=start and k % per_bank == 0, stop=False, skip_group_check=True)
                ins.then_inc(c.s_visit.sem, 1)

            def group(g, half, first):
                word = pe.value_load(c.words[0:1, bass.ds(g, 1)], min_val=0, max_val=NT << GRP)
                tile = word >> GRP
                pe.wait_ge(c.s_sel.sem, g + (sel0 + 1))
                for j in range(GS):
                    pe.wait_ge(c.s_hot.sem, g * GS + (hot0 + j + 1))
                    if first and j == 0:
                        products(j, half, True, None)
                        continue
                    begins = (word >> j) & 1
                    with pe.If(begins == 1):
                        with pe.If(heavy == 1):
                            leave_rest(within_tiles(tile))
                        products(j, half, True, tile)
                    with pe.Else():
                        products(j, half, False, None)
                    tile = tile + begins

            group(0, 0, True)
            group(1, 1, False)
            with pe.Fori(1, NG // 2) as it:
                for half in range(2):
                    group(it * 2 + half, half, False)
            with pe.If(heavy == 1):
                leave_rest(NT - 1)

        @block.scalar
        def _(act):
            heavy = act.value_load(c.heavy[0:1, 0:1], min_val=0, max_val=1)

            def bank(b, buf):
                n = min(per_bank, NT - b * per_bank)
                return nc.scalar.copy(buf[:, b * per_bank:b * per_bank + n, :],
                                      c.psum[b][:, 0:n * P].rearrange("p (k n) -> p k n", k=n))
            rest = c.rest[:, :].rearrange("p (k n) -> p k n", k=NT)
            for t in range(NT):
                end = act.value_load(c.ends[0:1, t:t + 1], min_val=1, max_val=NI)
                counts = c.at[:, :, t * P:(t + 1) * P]
                with act.If(heavy == 0):
                    act.wait_ge(c.s_visit.sem, end + vis0)
                    for b in range(NB):
                        bank(b, counts).then_inc(c.s_taken.sem, 1)
                with act.Else():
                    act.wait_ge(c.s_visit.sem, end + vis0)
                    for b in range(NB):
                        bank(b, counts).then_inc(c.s_round.sem, 1)
                        act.wait_ge(c.s_less.sem, t * NB + b + 1)
                        bank(b, rest).then_inc(c.s_taken.sem, 1)
                    act.wait_ge(c.s_taken.sem, tak0 + NB * (t + 1))
                    act.dma_start(c.rests[t, :, :], c.rest[:, :]).then_inc(c.s_rest_kept.sem, 16)
                    act.wait_ge(c.s_rest_kept.sem, 16 * (t + 1))
    c.s_load.n += 32
    c.s_pool.n += 1
    c.s_sel.n += NG
    c.s_hot.n += NI
    c.s_visit.n += NI
    c.s_taken.n += NB * NT


def phase_split(nc, c, source, loads, reload=False):
    RG = UN
    ring = c.raw[:, 1280:1280 + 2 * RG * D].rearrange("p (s t d) -> p s t d", s=2, t=RG)
    load0, dve0, pe0, act0, spl0 = (x.n for x in (c.s_load, c.s_dve, c.s_pe, c.s_scaled, c.s_split))
    row0 = [x.n for x in c.s_row]
    turns = NT // RG
    with nc.Block() as block:

        @block.sync
        def _(sp):
            for g in range(turns):
                if g >= 2:
                    sp.wait_ge(c.s_split.sem, spl0 + g - 1)
                sp.dma_start(ring[:, g % 2, :, :],
                             source[g * RG * P:(g + 1) * RG * P, :].rearrange("(t p) d -> p t d", p=P)
                             ).then_inc(c.s_row[g % 2].sem, 16)
            for dst, src in loads:
                sp.dma_start(dst, src).then_inc(c.s_load.sem, 16)
            sp.wait_ge(c.s_load.sem, load0 + 16 * len(loads))

        @block.tensor
        def _(pe):
            pe.wait_ge(c.s_dve.sem, dve0 + 1)
            nc.tensor.transpose(c.psum[7][0:1, 0:P], c.biggest[:, 0:1], c.ident[:, :]).then_inc(c.s_pe.sem, 1)
            pe.wait_ge(c.s_dve.sem, dve0 + 2)
            nc.tensor.matmul(c.psum[6][:, 0:1], c.ones[0:1, :], c.biggest[0:1, 1:2], start=True, stop=True
                             ).then_inc(c.s_pe.sem, 1)

        @block.vector
        def _(dve):
            ch = Chain(dve, c.s_dve)
            v = nc.vector
            ch.inc(v.tensor_reduce(c.biggest[:, 0:1], c.amax[:, :], AX.X, ALU.max))
            dve.wait_ge(c.s_pe.sem, pe0 + 1)
            ch.inc(v.tensor_reduce(c.biggest[0:1, 1:2], c.psum[7][0:1, 0:P], AX.X, ALU.max))
            dve.wait_ge(c.s_pe.sem, pe0 + 2)
            ch.step(v.tensor_scalar(c.biggest[:, 2:3], c.psum[6][:, 0:1], 1e-30, None, ALU.max))
            ch.step(v.tensor_single_scalar(c.scale_i[:, 0:1], c.biggest[:, 2:3].bitcast(I32), 0x7F800000,
                                           ALU.bitwise_and))
            ch.inc(v.tensor_scalar(c.scale_i[:, 1:2], c.scale_i[:, 0:1], -float(14 << 23), None, ALU.add))
            ch.step(v.tensor_scalar(c.scale_i[:, 2:3], c.scale_i[:, 0:1], -1.0, float(268 << 23), ALU.mult, ALU.add))
            for g in range(turns):
                dve.wait_ge(c.s_scaled.sem, act0 + g + 1)
                tiles = slice(g * RG, (g + 1) * RG)
                v.scalar_tensor_tensor(c.hs[:, tiles, D:2 * D], ring[:, g % 2, :, :], c.scale_i[:, 2:3].bitcast(F32),
                                       c.hs[:, tiles, 0:D], ALU.mult, ALU.subtract).then_inc(c.s_split.sem, 1)

        @block.scalar
        def _(act):
            act.wait_ge(c.s_dve.sem, dve0 + 6)
            for g in range(turns):
                act.wait_ge(c.s_row[g % 2].sem, row0[g % 2] + 16 * (g // 2 + 1))
                nc.scalar.activation(c.hs[:, g * RG:(g + 1) * RG, 0:D], ring[:, g % 2, :, :], ACT.Copy,
                                     scale=c.scale_i[:, 2:3].bitcast(F32)).then_inc(c.s_scaled.sem, 1)
            if reload:
                src, dst = counts_parts(c)[0]
                act.dma_start(dst, src).then_inc(c.s_back[0].sem, 16)
    c.s_load.n += 16 * len(loads)
    c.s_pe.n += 2
    c.s_scaled.n += turns
    c.s_split.n += turns
    for k in range(2):
        c.s_row[k].n += 16 * ((turns + 1 - k) // 2)


FIRST, CONV, CONV_LAST, SAGE, SAGE_LAST = range(5)


def phase_dense(nc, c, kind, layer, source, target):
    sage = kind in (SAGE, SAGE_LAST)
    sums = kind != FIRST
    linear = kind != CONV_LAST
    own = kind == FIRST or sage
    raw = c.raw

    def ring(start, width):
        return raw[:, start:start + 2 * width].rearrange("p (s d) -> p s d", s=2)

    w = raw[:, 0:1024].rearrange("p (k n) -> p k n", k=2)
    bias = raw[:, 1024:1280]
    at = 1280
    row, tmp, y = ring(at, D), ring(at + 2 * D, D), ring(at + 4 * D, D)
    xt, out = ring(at + 6 * D, 2 * D), ring(at + 10 * D, D)
    scaled = tmp if kind == FIRST else row
    NK = 4 if sage else 2
    agg0, half0, post0, xs0, tr0, xt0, lin0, out0 = (x.n for x in (
        c.s_agg, c.s_half, c.s_post, c.s_scaled, c.s_tr, c.s_xt, c.s_lin, c.s_out))
    row0, sent0 = [x.n for x in c.s_row], [x.n for x in c.s_sent]
    dve0 = c.s_dve.n
    low0 = c.s_low.n
    rest0, used0, back0 = c.s_rest.n, c.s_rest_used.n, [x.n for x in c.s_back]
    reload = kind == SAGE and layer == 0
    BASE = 7
    ready, ready0 = (c.s_low, low0) if sage else (c.s_scaled, xs0)
    factor = {CONV: c.dinv, CONV_LAST: c.dinv, SAGE: c.ideg, SAGE_LAST: c.ideg, FIRST: c.dinv}[kind]
    with nc.Block() as block:

        @block.gpsimd
        def _(pool):
            if sums:
                heavy = pool.value_load(c.heavy[0:1, 0:1], min_val=0, max_val=1)
                with pool.If(heavy == 1):
                    for m in range(NT):
                        if m:
                            pool.wait_ge(c.s_rest_used.sem, used0 + m)
                        pool.dma_start(c.rest[:, :], c.rests[m, :, :]).then_inc(c.s_rest.sem, 16)

        @block.vector
        def _(dve):
            v = nc.vector
            if sums:
                v.tensor_scalar(c.factor[:, :], factor[:, :], c.scale_i[:, 1:2].bitcast(F32), None, ALU.mult
                                ).then_inc(c.s_dve.sem, 1)
                dve.wait_ge(c.s_dve.sem, dve0 + 1)

            def post(m):
                dve.wait_ge(c.s_half.sem, half0 + m + 1)
                if m >= 2:
                    if not linear:
                        dve.wait_ge(c.s_sent[m % 2].sem, sent0[m % 2] + 16 * (m // 2))
                    else:
                        dve.wait_ge(c.s_tr.sem if sage else c.s_scaled.sem, (tr0 if sage else xs0) + m - 1)
                v.scalar_tensor_tensor(y[:, m % 2, :], c.psum[m % 2][:, D:2 * D], c.factor[:, m:m + 1],
                                       tmp[:, m % 2, :], ALU.mult, ALU.add).then_inc(c.s_low.sem, 1)
                if not sage:
                    dve.wait_ge(c.s_low.sem, low0 + m + 1)
                    v.tensor_tensor(y[:, m % 2, :], y[:, m % 2, :], bias, ALU.add
                                    ).then_inc(c.s_post.sem, 1)

            for m in range(NT + 2):
                if sums and m < NT:
                    post(m)
                k = m - 2
                if linear and k >= 0:
                    dve.wait_ge(c.s_lin.sem, lin0 + k + 1)
                    if k >= 2:
                        dve.wait_ge(c.s_sent[k % 2].sem, sent0[k % 2] + 16 * (k // 2))
                    p = c.psum[4 + k % 2][:, 0:D]
                    if kind == SAGE:
                        v.tensor_scalar(out[:, k % 2, :], p, 0.0, None, ALU.max)
                    else:
                        v.tensor_copy(out[:, k % 2, :], p)
                    v.tensor_reduce(c.amax[:, k:k + 1], p, AX.X, ALU.max, apply_absolute_value=True
                                    ).then_inc(c.s_out.sem, 1)

        @block.scalar
        def _(act):
            for m in range(NT + 1):
                if reload and 1 <= m + 1 < NT // UN:
                    src, dst = counts_parts(c)[m + 1]
                    act.dma_start(dst, src).then_inc(c.s_back[m + 1].sem, 16)
                if sums and m < NT:
                    act.wait_ge(c.s_agg.sem, agg0 + m + 1)
                    if m == 0:
                        act.wait_ge(c.s_dve.sem, dve0 + 1)
                    elif m >= 2:
                        act.wait_ge(c.s_low.sem, low0 + m - 1)
                    nc.scalar.activation(tmp[:, m % 2, :], c.psum[m % 2][:, 0:D], ACT.Copy,
                                         scale=c.factor[:, m:m + 1]).then_inc(c.s_half.sem, 1)
                if m < NT and linear and not sage:
                    if kind == FIRST:
                        act.wait_ge(c.s_row[m % 2].sem, row0[m % 2] + 16 * (m // 2 + 1))
                    else:
                        act.wait_ge(c.s_post.sem, post0 + m + 1)
                    if m >= 2:
                        act.wait_ge(c.s_tr.sem, tr0 + m - 1)
                    nc.scalar.activation(scaled[:, m % 2, :], (row if kind == FIRST else y)[:, m % 2, :], ACT.Copy,
                                         scale=c.dinv[:, m:m + 1]).then_inc(c.s_scaled.sem, 1)
                k = m - 1
                if linear and k >= 0:
                    act.wait_ge(c.s_tr.sem, tr0 + k + 1)
                    if k >= 2:
                        act.wait_ge(c.s_lin.sem, lin0 + k - 1)
                    nc.scalar.copy(xt[:, k % 2, 0:NK * P], c.psum[2 + k % 2][:, 0:NK * P]).then_inc(c.s_xt.sem, 1)

        @block.tensor
        def _(pe):
            if sums:
                heavy = pe.value_load(c.heavy[0:1, 0:1], min_val=0, max_val=1)

            def aggregate(m, slot, first):
                if not first:
                    pe.wait_ge(c.s_low.sem, m + (low0 - 1))
                    pe.wait_ge(c.s_half.sem, m + (half0 - 1))

                def add(lhs, k, start=False):
                    return nc.tensor.matmul(c.psum[slot][:, :], lhs, c.hs[:, k, :], start=start, stop=False,
                                            skip_group_check=True)
                for k in range(NT - 1):
                    add(c.at[:, k, bass.ds(m * P, P)], k, k == 0)
                with pe.If(heavy == 1):
                    pe.wait_ge(c.s_rest.sem, m * 16 + (rest0 + 16))
                    for k in range(NT):
                        ins = add(c.rest[:, k * P:(k + 1) * P], k)
                    ins.then_inc(c.s_rest_used.sem, 1)
                ins = add(c.at[:, NT - 1, bass.ds(m * P, P)], NT - 1)
                if not sage:
                    ins = nc.tensor.matmul(c.psum[slot][:, :], c.ident16[:, :],
                                           c.hs[:, bass.ds(m, 1), :].rearrange("p o d -> p (o d)"),
                                           start=False, stop=False, skip_group_check=True)
                ins.then_inc(c.s_agg.sem, 1)

            def transposes(m, slot, first):
                if own and sage:
                    pe.wait_ge(c.s_row[slot].sem, row_turn(m) * 16 + row0[slot] + 16)
                pe.wait_ge(ready.sem, m + (ready0 + 1))
                if not first:
                    pe.wait_ge(c.s_xt.sem, m + (xt0 - 1))
                for k in range(NK):
                    src = (row if k < 2 else y) if sage else scaled
                    ins = nc.tensor.transpose(c.psum[2 + slot][:, k * P:(k + 1) * P],
                                              src[:, slot, (k % 2) * P:(k % 2 + 1) * P], c.ident[:, :])
                ins.then_inc(c.s_tr.sem, 1)

            def product(m, slot, first):
                pe.wait_ge(c.s_xt.sem, m + (xt0 + 1))
                if not first:
                    pe.wait_ge(c.s_out.sem, m + (out0 - 1))
                for k in range(NK):
                    ins = nc.tensor.matmul(c.psum[4 + slot][:, 0:D], xt[:, slot, k * P:(k + 1) * P],
                                           w[:, k % 2, (k // 2) * D:(k // 2 + 1) * D],
                                           start=k == 0, stop=not sage and k == NK - 1)
                if sage:
                    ins = nc.tensor.matmul(c.psum[4 + slot][:, 0:D], c.ones[0:1, :], bias[0:1, :],
                                           start=False, stop=True)
                ins.then_inc(c.s_lin.sem, 1)

            def row_turn(m):
                return Turn.now if not isinstance(m, int) else m // 2

            def step(m, early):
                if sums and m < NT:
                    aggregate(m, m % 2, m < 2)
                if linear and 1 <= m <= NT:
                    transposes(m - 1, (m - 1) % 2, m - 1 < 2)
                if linear and m >= 2:
                    product(m - 2, m % 2, m - 2 < 2)

            def loop_step(base, it, s):
                m = it * 2 + (base + s)
                par = (base + s) % 2
                if sums:
                    aggregate(m, par, False)
                if linear:
                    Turn.now = it + (base + s - 1) // 2
                    transposes(it * 2 + (base + s - 1), 1 - par, False)
                    product(it * 2 + (base + s - 2), par, False)

            for m in range(BASE):
                if reload and m % UN == 0:
                    pe.wait_ge(c.s_back[m // UN].sem, back0[m // UN] + 16)
                step(m, True)
            if reload:
                for k in range(-(-BASE // UN), NT // UN):
                    pe.wait_ge(c.s_back[k].sem, back0[k] + 16)
            with pe.Fori(0, (NT - BASE) // 2) as it:
                for s in range(2):
                    loop_step(BASE, it, s)
            for m in (NT, NT + 1):
                step(m, False)

        @block.sync
        def _(sp):
            def load(m):
                if m >= 2:
                    sp.wait_ge((c.s_tr if sage else c.s_scaled).sem, (tr0 if sage else xs0) + m - 1)
                sp.dma_start(row[:, m % 2, :], source[m * P:(m + 1) * P, :]).then_inc(c.s_row[m % 2].sem, 16)

            def send(m):
                if linear:
                    sp.wait_ge(c.s_out.sem, out0 + m + 1)
                else:
                    sp.wait_ge(c.s_post.sem, post0 + m + 1)
                sp.dma_start(target[m * P:(m + 1) * P, :], (out if linear else y)[:, m % 2, :]
                             ).then_inc(c.s_sent[m % 2].sem, 16)
            if own:
                load(0)
            for m in range(NT + 2):
                if own and m + 1 < NT:
                    load(m + 1)
                if linear and m >= 2:
                    send(m - 2)
                if not linear and m < NT:
                    send(m)
            for k in range(2):
                sp.wait_ge(c.s_sent[k].sem, sent0[k] + 16 * ((NT + 1 - k) // 2))
    if reload:
        for x in c.s_back:
            x.n += 16
    if sums:
        c.s_rest.n += 16 * NT
        for x in (c.s_agg, c.s_half, c.s_low, c.s_rest_used):
            x.n += NT
        if not sage:
            c.s_post.n += NT
        c.s_dve.n += 1
    if linear:
        for x in (c.s_tr, c.s_xt, c.s_lin, c.s_out):
            x.n += NT
        if not sage:
            c.s_scaled.n += NT
    for k in range(2):
        if own:
            c.s_row[k].n += 16 * ((NT + 1 - k) // 2)
        c.s_sent[k].n += 16 * ((NT + 1 - k) // 2)


def weights_view(c):
    return c.raw[:, 0:1024].rearrange("p (k n) -> p k n", k=2)


def bias_view(c):
    return c.raw[:, 1024:1280]


def phase_spill(nc, c, pairs):
    with nc.Block() as block:

        @block.sync
        def _(sp):
            for dst, src in pairs:
                sp.dma_start(dst, src).then_inc(c.s_store.sem, 16)
            sp.wait_ge(c.s_store.sem, c.s_store.n + 16 * len(pairs))
    c.s_store.n += 16 * len(pairs)


def tiles_view(buf):
    return buf.rearrange("(t p) d -> p t d", p=P)


def layer_convolutions(nc, c):
    ins = c.ins
    with ExitStack() as ctx:
        dense_memory(nc, ctx, c, "conv")
        phase_build_counts(nc, c)
        w, b = weights_view(c), bias_view(c)
        phase_load(nc, c, [(w[:, :, 0:D], halves(ins["L0_gnn_W1"]))] +
                   [(b, row_of(ins["L0_gnn_b1"]))])
        phase_dense(nc, c, FIRST, 0, c.xbuf, c.hbuf[0])
        for k in range(2):
            phase_split(nc, c, c.hbuf[k % 2],
                        [(w[:, :, 0:D], halves(ins[f"L0_gnn_W{k + 2}"])), (b, row_of(ins[f"L0_gnn_b{k + 1}"]))])
            phase_dense(nc, c, CONV, k, None, c.hbuf[1 - k % 2])
        phase_split(nc, c, c.hbuf[0], [(b, row_of(ins["L0_gnn_b3"]))])
        phase_dense(nc, c, CONV_LAST, 2, None, c.hbuf[1])
        with nc.Block() as block:

            @block.sync
            def _(sp):
                sp.wait_ge(c.s_keep.sem, 16 * len(counts_parts(c)))
        c.s_keep.n += 16 * len(counts_parts(c))


def counts_parts(c):
    width = UN * P
    return [(c.counts[g, :, :, :], c.at[:, :, g * width:(g + 1) * width]) for g in range(NT // UN)]


def layer_relations(nc, c):
    ins = c.ins
    with ExitStack() as ctx:
        edge_memory(nc, ctx, c, "rel")
        m = Core()
        tmp = c.tmp[:, :, :].rearrange("p s d -> p (s d)")
        m.rel = tmp[:, 0:2 * D].rearrange("p (k d) -> p k d", k=2)
        m.rel_t = tmp[:, 2 * D:2 * D + 2 * R].rearrange("p (k r) -> p k r", k=2)
        m.wide = ctx.enter_context(nc.sbuf_tensor("r_wide", [P, 2, P], F32))
        m.rel_score = ctx.enter_context(nc.sbuf_tensor("r_score", [P, R], F32))
        m.by_rel = ctx.enter_context(nc.sbuf_tensor("r_by_rel", [P, NIP], F32))
        m.junk = ctx.enter_context(nc.sbuf_tensor("r_junk", [P, GRP, R], F32))
        phase_start(nc, c)
        phase_norm(nc, c, (c.xbuf, c.hbuf[1]),
                   [(c.col_dst[:, :], c.planes[0, :, :]),
                           (c.col_src8[:, :], c.planes[4, :, :].bitcast(I32)), (c.col_et[:, :], c.planes[2, :, :])] +
                   [(c.w[:, k, :].rearrange("p (r n) -> p r n", r=NREL),
                     ins["L1_gnn_weight"][:, k * P:(k + 1) * P, :].rearrange("r p n -> p r n")) for k in range(2)] +
                   [(c.bias[:, 0, :], row_of(ins["L1_gnn_gamma"])), (c.bias[:, 1, :], row_of(ins["L1_gnn_beta"]))])
        phase_relation_scores(nc, c, m)
        phase_relation_table(nc, c)
        phase_edges(nc, c, m, c.rtab, c.col_src8)
        phase_batch_norm(nc, c)
        phase_spill(nc, c, [(c.planes[5, :, :], m.by_rel[:, :])])
        phase_norm(nc, c, to_dram=c.xbuf, magnitudes=True)


def layer_sage(nc, c):
    ins = c.ins
    with ExitStack() as ctx:
        dense_memory(nc, ctx, c, "sage")
        w, b = weights_view(c), bias_view(c)
        for k in range(3):
            source = (c.xbuf, c.hbuf[0], c.hbuf[1])[k]
            target = (c.hbuf[0], c.hbuf[1], c.hbuf[0])[k]
            phase_split(nc, c, source, [(w[:, :, 0:D], halves(ins[f"L2_gnn_W{k}_self"])),
                                        (w[:, :, D:2 * D], halves(ins[f"L2_gnn_W{k}_neigh"])),
                                        (b, row_of(ins[f"L2_gnn_b{k}"]))], reload=k == 0)
            phase_dense(nc, c, SAGE if k < 2 else SAGE_LAST, k, source, target)


def layer_attention(nc, c, out):
    with ExitStack() as ctx:
        edge_memory(nc, ctx, c, "att")
        phase_start(nc, c)
        m = Core()

        def sb(name, shape, dt=F32):
            return ctx.enter_context(nc.sbuf_tensor(name, shape, dt))

        tmp = c.tmp[:, :, :].rearrange("p s d -> p (s d)")
        m.rel = tmp[:, 0:2 * D].rearrange("p (k d) -> p k d", k=2)
        m.rel_t = tmp[:, 2 * D:2 * D + 2 * R].rearrange("p (k r) -> p k r", k=2)
        m.rel_w = sb("m_rel_w", [P, 2, D])
        xt2 = c.xt2[:, :, :].rearrange("p s d -> p (s d)")
        m.wide = xt2[:, 0:2 * P].rearrange("p (q n) -> p q n", q=2)
        m.by_rel = xt2[:, 2 * P:2 * P + NIP]
        m.junk_dst = tmp[:, 0:GRP * P].rearrange("p (j n) -> p j n", j=GRP)
        m.cols = sb("m_cols", [P, 2, GRP])
        flat = c.h[:, :, :].rearrange("p t d -> p (t d)")
        m.dst_score = flat[:, 0:NT * P]
        m.lane_r = c.lane_r
        m.rel_hot = flat[:, NT * P:NT * P + 2 * GRP * R].rearrange("p (s r) -> p s r", r=R)
        m.by_dst, m.score, m.leak, m.expo, m.alpha = (
            sb("m_" + name, [P, 2, GRP]) for name in ("by_dst", "score", "leak", "expo", "alpha"))
        m.no_in = sb("m_no_in", [P, NT])
        m.xt3 = c.w[:, :, 4 * D:7 * D]
        phase_norm(nc, c, (c.xbuf, c.hbuf[0]),
                   [(c.col_dst[:, :], c.planes[0, :, :]), (c.col_et[:, :], c.planes[2, :, :]),
                           (c.col_src[:, :], c.planes[3, :, :].bitcast(I32)), (m.by_rel, c.planes[5, :, :])])
        phase_attention_weights(nc, c, m)
        phase_node_scores(nc, c, m)
        phase_to_table(nc, c, c.acc[:, :, 0:D + 4], c.ltab, D + R)
        phase_attention_edges(nc, c, m)
        phase_attention_linear(nc, c, m)
        phase_norm(nc, c, to_dram=out)


def row_of(v):
    return v.rearrange("(o d) -> o d", o=1).to_broadcast([P, D])


def build(nc, ins, out, stage=3):
    c = Core()
    c.ins = ins
    with ExitStack() as ctx:
        allocate(nc, ctx, c)
        with ExitStack() as first:
            edge_memory(nc, first, c, "prep")
            phase_start(nc, c)
            prepare(nc, c)
            phase_spill(nc, c, [(tiles_view(c.xbuf), c.x[:, :, :])])
        layer_convolutions(nc, c)
        layer_relations(nc, c)
        layer_sage(nc, c)
        layer_attention(nc, c, out)


NAMES = {"x": "x", "src": "src", "dst": "dst", "et200": "edge_type_200", "et8": "edge_type_8"}


def kernel(**inputs):
    import numpy as _np
    import concourse.bacc as _bacc
    from concourse import mybir as _mybir
    from concourse.bass_utils import run_bass_kernel_spmd as _run

    nc = _bacc.Bacc("TRN2", target_bir_lowering=False, num_devices=1)
    short = {v: k for k, v in NAMES.items()}
    arrays, args = {}, {}
    for name in inputs:
        a = _np.ascontiguousarray(inputs[name])
        arrays[f"in_{name}"] = a
        args[short.get(name, name)] = nc.dram_tensor(f"in_{name}", a.shape, _mybir.dt.from_np(a.dtype),
                                                     kind="ExternalInput").ap()
    out = nc.dram_tensor("out_0", (N, D), _mybir.dt.float32, kind="ExternalOutput").ap()
    build(nc, args, out)
    r = _run(nc, [arrays], core_ids=[0])
    return r.results[0]["out_0"]
```
